# Optimizing a Trainium2 kernel written in Bass

```python
import numpy as np
import jax
import jax.numpy as jnp

def _softmax(x, axis=-1):
    return jax.nn.softmax(x, axis=axis)

def _gelu(x):
    return jax.nn.gelu(x, approximate=True)

def _silu(x):
    return jax.nn.silu(x)

def _sigmoid(x):
    return jax.nn.sigmoid(x)

def _layernorm(x, axis=-1, eps=1e-05):
    m = jnp.mean(x, axis=axis, keepdims=True)
    v = jnp.var(x, axis=axis, keepdims=True)
    return (x - m) / jnp.sqrt(v + eps)

def _scatter_add(tgt, idx, src, axis=0):
    return tgt.at[idx].add(src)

def _segment_sum(src, seg, n):
    return jax.ops.segment_sum(src, seg, n)
kernel_name = 'mk_gnn_preln_d1_gnn_r8_646952'

def setup_inputs(seed: int=0):
    np.random.seed(seed)
    _w = jnp.asarray

    def _rec_inputs():
        import jax
        import jax.numpy as jnp
        _gk = jax.random.key(seed)
        x = -0.000202 + 1 * jax.random.normal(jax.random.fold_in(_gk, 1), (12500, 64), jnp.float32)
        src = jax.random.randint(jax.random.fold_in(_gk, 2), (200000,), 0, 12500, jnp.int32)
        dst = jax.random.randint(jax.random.fold_in(_gk, 3), (200000,), 0, 12500, jnp.int32)
        _o = jnp.argsort(dst, stable=True)
        src = src[_o]
        dst = dst[_o]
        edge_attr_64 = -8.16379e-05 + 0.999858 * jax.random.normal(jax.random.fold_in(_gk, 12), (200000, 64), jnp.float32)
        return (x, src, dst, edge_attr_64)
    x, src, dst, edge_attr_64 = _rec_inputs()

    def _L0_gnn_setup():
        import jax, jax.numpy as jnp
        import numpy as np
        N_NODES = 12500
        N_EDGES = 200000
        IN_SIZE = 64
        OUT_SIZE = 64
        N_HEADS = 2
        NEG_SLOPE = 0.2
        BN_EPS = 1e-05
        key = jax.random.key(seed)
        ks = jax.random.split(key, 8)
        atom = jax.random.normal(ks[0], (N_NODES, IN_SIZE), dtype=jnp.float32)
        bond = jax.random.normal(ks[1], (N_EDGES, IN_SIZE), dtype=jnp.float32)
        W = jax.random.normal(ks[2], (IN_SIZE, OUT_SIZE * N_HEADS), dtype=jnp.float32) * 0.1
        attn_l = jax.random.normal(ks[3], (N_HEADS, OUT_SIZE), dtype=jnp.float32) * 0.1
        attn_r = jax.random.normal(ks[4], (N_HEADS, OUT_SIZE), dtype=jnp.float32) * 0.1
        bn_gamma = jnp.ones((OUT_SIZE,), dtype=jnp.float32)
        bn_beta = jnp.zeros((OUT_SIZE,), dtype=jnp.float32)
        src = jax.random.randint(ks[5], (N_EDGES,), 0, N_NODES, dtype=jnp.int32)
        dst = jax.random.randint(ks[6], (N_EDGES,), 0, N_NODES, dtype=jnp.int32)
        return {'atom': atom, 'bond': bond, 'W': W, 'attn_l': attn_l, 'attn_r': attn_r, 'bn_gamma': bn_gamma, 'bn_beta': bn_beta, 'src': src, 'dst': dst}
    _L0_gnn_all = _L0_gnn_setup()
    _L0_gnn_in = {k: v for k, v in _L0_gnn_all.items() if k in ('W', 'attn_l', 'attn_r', 'bn_gamma', 'bn_beta')}
    del _L0_gnn_all
    return {'x': x, 'src': src, 'dst': dst, 'edge_attr_64': edge_attr_64, 'L0_gnn_W': _L0_gnn_in['W'], 'L0_gnn_attn_l': _L0_gnn_in['attn_l'], 'L0_gnn_attn_r': _L0_gnn_in['attn_r'], 'L0_gnn_bn_gamma': _L0_gnn_in['bn_gamma'], 'L0_gnn_bn_beta': _L0_gnn_in['bn_beta']}

def reference(x, src, dst, edge_attr_64, L0_gnn_W, L0_gnn_attn_l, L0_gnn_attn_r, L0_gnn_bn_gamma, L0_gnn_bn_beta):
    import jax
    import jax.numpy as jnp

    def _L0_gnn_ref(atom, bond, W, attn_l, attn_r, bn_gamma, bn_beta, src, dst):
        import jax, jax.numpy as jnp
        import numpy as np
        N_NODES = 12500
        N_EDGES = 200000
        IN_SIZE = 64
        OUT_SIZE = 64
        N_HEADS = 2
        NEG_SLOPE = 0.2
        BN_EPS = 1e-05
        N = atom.shape[0]
        H, D = attn_l.shape
        h_edge = ((atom[src] + bond) @ W).reshape(-1, H, D)
        h_node = (atom @ W).reshape(-1, H, D)
        el = jnp.einsum('ehd,hd->eh', h_edge, attn_l)
        er = jnp.einsum('nhd,hd->nh', h_node, attn_r)
        s = el + er[dst]
        s = jnp.where(s > 0, s, NEG_SLOPE * s)
        smax = jax.ops.segment_max(s, dst, num_segments=N)
        ex = jnp.exp(s - smax[dst])
        denom = jax.ops.segment_sum(ex, dst, num_segments=N)
        alpha = ex / denom[dst]
        ft = jax.ops.segment_sum(h_edge * alpha[..., None], dst, num_segments=N)
        h = ft.mean(axis=1)
        mu = h.mean(axis=0)
        var = h.var(axis=0)
        h = (h - mu) / jnp.sqrt(var + BN_EPS) * bn_gamma + bn_beta
        h = jax.nn.relu(h)
        return h
    h = jnp.maximum(_layernorm(x, axis=-1), 0.0)
    x = x + _L0_gnn_ref(h, edge_attr_64, L0_gnn_W, L0_gnn_attn_l, L0_gnn_attn_r, L0_gnn_bn_gamma, L0_gnn_bn_beta, src, dst)
    return x

_drawn_inputs = setup_inputs


def setup_inputs(seed=0):
    import zlib

    import numpy as np

    out = dict(_drawn_inputs(seed))
    spreads = {'L0_gnn_bn_gamma': (1.0, 0.2), 'L0_gnn_bn_beta': (0.0, 0.1)}
    factors = {}
    for name, (base, spread) in spreads.items():
        noise = np.random.default_rng([zlib.crc32(name.encode()), seed]).standard_normal(out[name].shape)
        drawn = base * np.exp(spread * noise) if base else spread * noise
        out[name] = jnp.asarray(drawn.astype(out[name].dtype))
    for name, factor in factors.items():
        out[name] = (out[name] * factor).astype(out[name].dtype)
    return out
```

```python
import concourse.bass as bass
from concourse import mybir
from contextlib import ExitStack

N, E, F, H = 12500, 200000, 64, 2
P = 128
EPP = 2
GROUP = P * EPP
WIN = 32
CG = 16
CT = CG * EPP
CHUNK = CG * GROUP
NCH = -(-E // CHUNK)
NGR = -(-E // GROUP)
NGP = NCH * CG
RP = 112
RG = NGP // RP
assert RP * RG == NGP
FULL = E // GROUP
TAIL = E - FULL * GROUP
assert TAIL % EPP == 0 and FULL + 1 == NGR
EPAD = NGP * GROUP
NACC = N + WIN
NP_, NB = 125, 100
assert NP_ * NB == N
PS = (0, 112, 125)
EW_ROWS = 12512
F1 = F + 1
BIG = 1.0e37
NEG_SLOPE, LN_EPS, BN_EPS = 0.2, 1e-5, 1e-5
ZB = 3
NZ = -(-NB // ZB)


def gnn_kernel(nc, x, src, dst, ea, W, attn_l, attn_r, gamma, beta, out):
    f32, i32 = mybir.dt.float32, mybir.dt.int32
    ALU, ACT, AX = mybir.AluOpType, mybir.ActivationFunctionType, mybir.AxisListType

    def view(ap, dims, off=0):
        return bass.AP(ap.tensor, ap.offset + off, [list(ap.ap[0])] + [list(d) for d in dims])

    with ExitStack() as ctx:
        def sb(name, shape, dt=f32):
            return ctx.enter_context(nc.sbuf_tensor(name, shape, dt))

        def sem(name):
            return ctx.enter_context(nc.semaphore(name))

        h_tab = nc.dram_tensor("h_tab", (N, F), f32, kind="Internal").ap()
        er_tab = nc.dram_tensor("er_tab", ((EW_ROWS + WIN) * H,), f32, kind="Internal").ap()
        er_win = nc.dram_tensor("er_win", (EW_ROWS, WIN * H), f32, kind="Internal").ap()
        dst_pad = nc.dram_tensor("dst_pad", (EPAD + 2,), i32, kind="Internal").ap()

        acc = sb("acc", [P, H, NACC])
        accf = acc[:, :, :].rearrange("p h n -> p (h n)")
        work = sb("work", [P, 5, CT * F])
        gat = [work[:, q, :].rearrange("p (t f) -> p t f", f=F) for q in range(2)]
        edge = [work[:, 2 + q, :].rearrange("p (t f) -> p t f", f=F) for q in range(3)]
        zt = view(work[:, 0, :], [[F, NB], [1, F]])
        onehot = sb("onehot", [P, 2, CT, WIN])
        scaled = sb("scaled", [P, CT, H, WIN])
        eT = sb("eT", [P, CG, P])
        ohT = sb("ohT", [P, CG // 2, P])
        srcI = sb("srcI", [P, NGP, EPP], i32)
        rel = sb("rel", [P, NGP, EPP])
        er_bd = sb("er_bd", [P, NGP, EPP, H])
        ident = sb("ident", [P, P])
        ones = sb("ones", [P, P])
        iota_i = sb("iota_i", [P, WIN], i32)
        iota = sb("iota", [P, WIN])
        neg1 = sb("neg1", [1, 1], i32)
        wlr = sb("wlr", [P, 2 * H])
        wl2 = sb("wl2", [P, EPP * H])
        wrb = sb("wrb", [P, H, F])
        wz = sb("wz", [F1, H, F1])
        gb = sb("gb", [P, 2, F])
        R2 = H * CG
        s_raw = sb("s_raw", [P, H, CG, EPP])
        s_lr = sb("s_lr", [P, H, CG, EPP])
        sdif = sb("sdif", [P, H, CG, EPP])
        p_e = sb("p_e", [P, H, CT])
        drow2_i = sb("drow2_i", [R2, GROUP + 2], i32)
        drow = sb("drow", [R2, GROUP + 2])
        pen = sb("pen", [R2, GROUP + 1])
        pen_first = sb("pen_first", [R2, GROUP])
        pen_last = sb("pen_last", [R2, GROUP])
        fw = sb("fw", [R2, GROUP])
        bw = sb("bw", [R2, GROUP])
        mx = sb("mx", [R2, GROUP])
        rowsum = sb("rowsum", [R2, 6])
        tail_in = sb("tail_in", [1, H, CG + 1])
        head_in = sb("head_in", [1, H, CG + 1])
        cin = sb("cin", [1, H, CG])
        cout = sb("cout", [1, H, CG])
        cc = sb("cc", [R2, 2])
        fmax = sb("fmax", [1, H, 1])
        fdif = sb("fdif", [1, H])
        fexp = sb("fexp", [1, H])
        rden = sb("rden", [P, ZB, H])
        TAILC, HEADC, CONNF, LINKF, CONNB, LINKB = range(6)

        xln = view(accf, [[F, NB], [1, F]])
        tln = view(accf, [[F, NB], [1, F]], NB * F)
        o = 2 * NB * F
        srow_i = view(accf, [[GROUP, RG], [1, GROUP]], o).bitcast(i32)
        srow = view(accf, [[GROUP, RG], [1, GROUP]], o + RG * GROUP)
        drw_i = view(accf, [[GROUP, RG], [1, GROUP]], o + 2 * RG * GROUP).bitcast(i32)
        drw = view(accf, [[GROUP, RG], [1, GROUP]], o + 3 * RG * GROUP)
        erg = view(accf, [[WIN * H, RG], [1, WIN * H]], o + 4 * RG * GROUP)
        taken = [o + 4 * RG * GROUP + RG * WIN * H]

        def lend(*dims):
            size = 1
            for d in dims:
                size *= d
            taken[0] += size
            assert taken[0] <= H * NACC
            step_, ap = size, []
            for d in dims:
                step_ //= d
                ap.append([step_, d])
            return view(accf, ap, taken[0] - size)

        padc = lend(EPAD + 1 - E)[0:1].bitcast(i32)
        zrow = lend((EW_ROWS + WIN - N) * H)[0:1]
        Wd, alb, arb, wtmp = (lend(H * F) for _ in range(4))
        wrB = lend(H, P)[0:F]
        ln_a, ln_b, er = lend(NB), lend(NB), lend(NB, H)
        quarter = lend(RP, EPP)
        st = view(accf, [[F, 6], [1, F]], 2 * NB * F)
        zw = view(scaled[:, 0, 0, :], [[H * F, ZB], [F, H], [1, F]])
        bases = lend(NGP)[96:97].bitcast(i32)

        pt = [ctx.enter_context(nc.psum_tensor(f"pt{i}", [P, 512], f32)) for i in range(2)]
        p_s = ctx.enter_context(nc.psum_tensor("p_s", [P, 512], f32))
        p_m = ctx.enter_context(nc.psum_tensor("p_m", [P, 512], f32))
        p_r = ctx.enter_context(nc.psum_tensor("p_r", [P, 512], f32))
        p_q = ctx.enter_context(nc.psum_tensor("p_q", [P, 512], f32))
        po = [ctx.enter_context(nc.psum_tensor(f"po{i}", [P, 512], f32)) for i in range(2)]
        S_ps = p_s[:, 0:CT * H]
        M_ps = p_m[:, 0:CT * H]
        sT_ps = p_r[0:R2, 0:GROUP]
        row_ps = p_q[0:1, 0:6 * R2]
        cc_ps = p_q[0:R2, 200:202]
        fb_ps = p_m[0:F1, 256:256 + H]

        s_x, s_src, s_w, s_dpad, s_drw = sem("s_x"), sem("s_src"), sem("s_w"), sem("s_dpad"), sem("s_drw")
        s_const, s_pz, s_gp = sem("s_const"), sem("s_pz"), sem("s_gp")
        s_bases, s_htab, s_ertab, s_erwin, s_erg = sem("s_bases"), sem("s_htab"), sem("s_ertab"), sem("s_erwin"), sem("s_erg")
        s_rows, s_rt, s_srcI = sem("s_rows"), sem("s_rt"), sem("s_srcI")
        s_pq, s_aq = sem("s_pq"), sem("s_aq")
        s_v = sem("s_v")
        s_b = [sem(f"s_b{i}") for i in range(3)]
        s_d = sem("s_d")
        s_g = [sem("s_g0"), sem("s_g1")]
        s_E, s_oh, s_tr, s_te, s_S, s_Sc = sem("s_E"), sem("s_oh"), sem("s_tr"), sem("s_te"), sem("s_S"), sem("s_Sc")
        s_drc, s_leaky, s_sT, s_rs, s_row, s_cc, s_ccp = (sem("s_drc"), sem("s_leaky"), sem("s_sT"), sem("s_rs"), sem("s_row"),
                                                       sem("s_cc"), sem("s_ccp"))
        s_fd, s_fx, s_fb, s_mx, s_M, s_sd, s_p = (sem("s_fd"), sem("s_fx"), sem("s_fb"), sem("s_mx"), sem("s_M"),
                                                  sem("s_sd"), sem("s_p"))
        s_ohp, s_o, s_acc = sem("s_ohp"), sem("s_o"), sem("s_acc")
        s_z, s_zv, s_bn, s_bp, s_ba, s_xe, s_y, s_out = (sem("s_z"), sem("s_zv"), sem("s_bn"), sem("s_bp"), sem("s_ba"),
                                                         sem("s_xe"), sem("s_y"), sem("s_out"))

        s_rows_f = [sem("s_rows_src"), sem("s_rows_dst")]
        s_rte, s_wr, s_wrp, s_ergc = sem("s_rte"), sem("s_wr"), sem("s_wrp"), sem("s_ergc")
        tln_rep = view(accf, [[1, RG * H * P]], NB * F)

        def base_regs(c):
            return nc.values_load_multi_w_load_instructions(
                bases[0:1, c * CG:(c + 1) * CG], engines=[mybir.EngineType.DVE], min_val=0, max_val=N)[1]

        def groups_in(c):
            return min(CG, NGR - c * CG)

        def gathers_upto(c):
            return sum(EPP * groups_in(i) for i in range(c % 2, c + 1, 2))

        def bond_dmas(c):
            return 2 if (c + 1) * CHUNK > E else 1

        def bonds_upto(c):
            return sum(bond_dmas(i) for i in range(c % 3, c + 1, 3))

        NRT = RG * EPP
        QS = [(0, 25), (25, 50), (50, 75), (75, 100)]

        block = ctx.enter_context(nc.Block())

        @block.sync
        def _(sp):
            sp.wait_ge(s_pz, 1)
            fullg = FULL // RP
            rest = FULL - fullg * RP
            sp.dma_start(srow_i[0:RP, 0:fullg, :],
                         src[0:fullg * RP * GROUP].rearrange("(g p e) -> p g e", p=RP, e=GROUP)).then_inc(s_src, 16)
            sp.dma_start(srow_i[0:rest, fullg, :],
                         src[fullg * RP * GROUP:FULL * GROUP].rearrange("(p e) -> p e", e=GROUP)).then_inc(s_src, 16)
            sp.dma_start(srow_i[rest:rest + 1, fullg, 0:TAIL],
                         src[FULL * GROUP:E].rearrange("(p e) -> p e", p=1)).then_inc(s_src, 16)
            sp.dma_start(dst_pad[1:1 + E].rearrange("(a b) -> a b", a=16),
                         dst[0:E].rearrange("(a b) -> a b", a=16)).then_inc(s_dpad, 16)
            sp.wait_ge(s_gp, 1)
            sp.dma_start(dst_pad[1 + E:EPAD + 2].rearrange("(p e) -> p e", p=1), padc[:, :]).then_inc(s_dpad, 16)
            sp.dma_start(dst_pad[0:1].rearrange("(p e) -> p e", p=1), neg1[:, :]).then_inc(s_dpad, 16)
            sp.wait_ge(s_dpad, 48)
            sp.dma_start(drw_i[0:RP], dst_pad[1:1 + EPAD].rearrange("(g p e) -> p g e", p=RP, e=GROUP)).then_inc(s_drw, 16)
            with nc.allow_non_contiguous_dma(reason="first dst of each group"):
                sp.dma_start(bases[:, :], bass.AP(dst_pad.tensor, 1, [[1, 1], [GROUP, NGP], [1, 1]])).then_inc(s_bases, 16)

            def load_chunk(c):
                q = c % 3
                if c >= 3:
                    sp.wait_ge(s_o, 2 * (c - 2))
                ng = min(CG, FULL - c * CG)
                sp.dma_start(edge[q].rearrange("p (g j) f -> p g (j f)", j=EPP)[:, 0:ng, :],
                             ea[c * CHUNK:c * CHUNK + ng * GROUP, :].rearrange("(g p j) f -> p g (j f)", p=P, j=EPP)
                             ).then_inc(s_b[q], 16)
                if bond_dmas(c) == 2:
                    sp.dma_start(edge[q].rearrange("p (g j) f -> p g (j f)", j=EPP)[0:TAIL // EPP, ng, :],
                                 ea[FULL * GROUP:E, :].rearrange("(p j) f -> p (j f)", j=EPP)).then_inc(s_b[q], 16)
                if c >= 1:
                    sp.wait_ge(s_drc, c)
                for hd in range(H):
                    sp.dma_start(drow2_i[hd * CG:(hd + 1) * CG, :],
                                 bass.AP(dst_pad.tensor, c * CHUNK, [[GROUP, CG], [1, GROUP + 2]])).then_inc(s_d, 16)

            load_chunk(0)
            for a, (p0, p1) in enumerate(zip(PS, PS[1:])):
                if a == 0:
                    sp.wait_ge(s_rows, 1)
                sp.dma_start(h_tab.rearrange("(p b) f -> p b f", b=NB)[p0:p1], xln[p0:p1]).then_inc(s_htab, 16)
            sp.wait_ge(s_rows, 2)
            for p0, p1 in zip(PS, PS[1:]):
                sp.dma_start(er_tab[0:N * H].rearrange("(p b) -> p b", b=NB * H)[p0:p1],
                             er[p0:p1].rearrange("p b h -> p (b h)")).then_inc(s_ertab, 16)
            sp.dma_start(er_tab[N * H:(EW_ROWS + WIN) * H].rearrange("(p e) -> p e", p=1), zrow[:, :]).then_inc(s_ertab, 16)
            sp.wait_ge(s_ertab, 48)
            sp.dma_start(er_win[:, :], bass.AP(er_tab.tensor, 0, [[H, EW_ROWS], [1, WIN * H]])).then_inc(s_erwin, 16)
            for c in range(1, NCH):
                load_chunk(c)
            sp.wait_ge(s_z, NZ)
            for p0, p1 in zip(PS, PS[1:]):
                sp.dma_start(xln[p0:p1], x.rearrange("(p b) f -> p b f", b=NB)[p0:p1]).then_inc(s_xe, 16)
            for i, (b0, b1) in enumerate(QS):
                sp.wait_ge(s_y, i + 1)
                for p0, p1 in zip(PS, PS[1:]):
                    sp.dma_start(out.rearrange("(p b) f -> p b f", b=NB)[p0:p1, b0:b1], zt[p0:p1, b0:b1]).then_inc(s_out, 16)
            sp.wait_ge(s_htab, 32)
            sp.wait_ge(s_erwin, 16)
            sp.wait_ge(s_out, 16 * 2 * len(QS))

        @block.gpsimd
        def _(pool):
            nc.gpsimd.memset(padc[:, :], N).then_inc(s_const, 1)
            nc.gpsimd.memset(neg1[:, :], -1).then_inc(s_const, 1)
            nc.gpsimd.memset(ident[:, :], 0.0).then_inc(s_const, 1)
            nc.gpsimd.iota(iota_i[:, :], [[1, WIN]], base=0, channel_multiplier=0).then_inc(s_const, 1)
            pool.wait_ge(s_const, 4)
            nc.gpsimd.affine_select(out=ident[:, :], in_=ident[:, :], compare_op=ALU.not_equal, fill=1.0, base=0,
                                    pattern=[[-1, P]], channel_multiplier=1).then_inc(s_gp, 1)

            def gather(c):
                q = c % 2
                if c >= 2:
                    pool.wait_ge(s_E, c - 1)
                for g in range(groups_in(c)):
                    for j in range(EPP):
                        k = c * CG + g
                        pool.indirect_dma_start(out=gat[q][:, g * EPP + j, :], out_offset=None, in_=h_tab,
                                                in_offset=bass.IndirectOffsetOnAxis(ap=srcI[:, k, j:j + 1], axis=0)
                                                ).then_inc(s_g[q], 16)

            pool.wait_ge(s_srcI, 1)
            pool.wait_ge(s_htab, 32)
            gather(0)
            gather(1)
            pool.wait_ge(s_erwin, 16)
            pool.wait_ge(s_drw, 16)
            for g in range(RG):
                pool.indirect_dma_start(out=erg[0:RP, g, :], out_offset=None, in_=er_win,
                                        in_offset=bass.IndirectOffsetOnAxis(ap=drw_i[0:RP, g, 0:1], axis=0)
                                        ).then_inc(s_erg, 16)
            for c in range(2, NCH):
                gather(c)

        @block.scalar
        def _(act):
            for p0, p1 in zip(PS, PS[1:]):
                act.dma_start(xln[p0:p1], x.rearrange("(p b) f -> p b f", b=NB)[p0:p1]).then_inc(s_x, 16)
            for a in range(2):
                act.dma_start(Wd[a * F:(a + 1) * F, :], W[:, :]).then_inc(s_w, 16)
            for t, v in ((alb[:, :], attn_l), (arb[:, :], attn_r)):
                act.dma_start(t, bass.AP(v.tensor, 0, [[0, P], [1, H * F]])).then_inc(s_w, 16)
            for i, v in enumerate((gamma, beta)):
                act.dma_start(gb[:, i, :], bass.AP(v.tensor, 0, [[0, P], [1, F]])).then_inc(s_w, 16)
            act.wait_ge(s_pq, 1)
            nc.scalar.activation(xln[0:NP_], tln[0:NP_], ACT.Square).then_inc(s_aq, 1)
            act.wait_ge(s_pq, 2)
            nc.scalar.activation(ln_b[0:NP_, :], ln_a[0:NP_, :], ACT.Sqrt).then_inc(s_aq, 1)

            n_tr = 0
            for c in range(NCH):
                for r in range(6):
                    n_tr += 1
                    act.wait_ge(s_tr, n_tr)
                    if r == 0 and c:
                        act.wait_ge(s_S, c)
                    dest = eT[:, 4 * r:4 * r + 4, :] if r < 4 else ohT[:, 4 * (r - 4):4 * (r - 4) + 4, :]
                    nc.scalar.activation(dest, pt[(n_tr - 1) % 2][:, :].rearrange("p (a b) -> p a b", b=P), ACT.Copy
                                         ).then_inc(s_te, 1)
                act.wait_ge(s_S, c + 1)
                if c:
                    act.wait_ge(s_leaky, c)
                nc.scalar.activation(s_raw[:, :, :, :].rearrange("p h g j -> p g j h"),
                                     S_ps.rearrange("p (g j h) -> p g j h", j=EPP, h=H), ACT.Copy).then_inc(s_Sc, 1)
                act.wait_ge(s_fd, c + 1)
                if c:
                    act.wait_ge(s_fb, c)
                nc.scalar.activation(fexp[:, :], fdif[:, :], ACT.Exp).then_inc(s_fx, 1)
                act.wait_ge(s_sd, c + 1)
                if c:
                    act.wait_ge(s_ohp, c)
                nc.scalar.activation(p_e[:, :, :], sdif[:, :, :, :].rearrange("p h g j -> p h (g j)"), ACT.Exp
                                     ).then_inc(s_p, 1)
            act.wait_ge(s_bn, 2)
            nc.scalar.activation(tln[0:NP_], zt[0:NP_], ACT.Square).then_inc(s_ba, 1)
            act.wait_ge(s_bn, 4)
            nc.scalar.activation(st[:, 4, :], st[:, 3, :], ACT.Sqrt).then_inc(s_ba, 1)

        @block.tensor
        def _(pe):
            mm = nc.tensor.matmul
            pe.wait_ge(s_gp, 1)
            n_rt = 0
            for arr, ready in ((srow, s_rows_f[0]), (drw, s_rows_f[1])):
                if arr is drw:
                    pe.wait_ge(s_wr, 1)
                    for hd in range(H):
                        m = mm(p_q[:, hd * F:(hd + 1) * F], wrB[:, hd, :], ident[0:F, 0:F], start=True, stop=True)
                    m.then_inc(s_wrp, 1)
                pe.wait_ge(ready, 1)
                for g in range(RG):
                    for j in range(EPP):
                        if n_rt >= 2:
                            pe.wait_ge(s_rte, n_rt - 1)
                        mm(pt[n_rt % 2][:, 0:RP], view(arr[0:RP], [[EPP, P]], g * GROUP + j), ident[0:RP, 0:RP],
                           start=True, stop=True).then_inc(s_rt, 1)
                        n_rt += 1
            pe.wait_ge(s_ergc, 1)
            for g in range(RG):
                for hd in range(H):
                    pe.wait_ge(s_rte, n_rt - 1)
                    mm(pt[n_rt % 2][:, 0:RP], tln_rep[0:RP, (g * H + hd) * P:(g * H + hd + 1) * P],
                       ident[0:RP, 0:RP], start=True, stop=True).then_inc(s_rt, 1)
                    n_rt += 1
            pe.wait_ge(s_rte, n_rt)

            n_tr = 0
            for c in range(NCH):
                q = c % 2
                pe.wait_ge(s_E, c + 1)
                for r in range(6):
                    if r == 4:
                        pe.wait_ge(s_oh, c + 1)
                    if n_tr >= 2:
                        pe.wait_ge(s_te, n_tr - 1)
                    for i in range(4):
                        if r < 4:
                            t0 = (4 * r + i) * EPP
                            a = edge[c % 3][:, t0:t0 + EPP, :].rearrange("p t f -> p (t f)")
                        else:
                            t0 = (4 * (r - 4) + i) * 4
                            a = onehot[:, q, t0:t0 + 4, :].rearrange("p t w -> p (t w)")
                        m = nc.tensor.transpose(pt[n_tr % 2][:, i * P:(i + 1) * P], a, ident[:, :])
                    m.then_inc(s_tr, 1)
                    n_tr += 1
                pe.wait_ge(s_te, n_tr)
                if c:
                    pe.wait_ge(s_Sc, c)
                for g in range(CG):
                    k = c * CG + g
                    if g % 2 == 0:
                        mm(S_ps[:, g * 4:g * 4 + 8], ohT[:, g // 2, :],
                           er_bd[:, k:k + 2, :, :].rearrange("p k j h -> p (k j h)"),
                           start=True, stop=False, skip_group_check=True)
                    m = mm(S_ps[:, g * 4:g * 4 + 4], eT[:, g, :], wl2[:, :], start=False, stop=True,
                           skip_group_check=True)
                m.then_inc(s_S, 1)
                pe.wait_ge(s_leaky, c + 1)
                for j in range(EPP):
                    m = mm(view(sT_ps, [[EPP, P]], j), s_lr[:, :, :, j].rearrange("p h g -> p (h g)"), ident[:, :],
                           start=True, stop=True)
                m.then_inc(s_sT, 1)
                pe.wait_ge(s_rs, c + 1)
                for i in range(6):
                    m = mm(row_ps[:, i * R2:(i + 1) * R2], rowsum[:, i:i + 1], ident[0:R2, 0:R2], start=True, stop=True)
                m.then_inc(s_row, 1)
                pe.wait_ge(s_cc, c + 1)
                for i, t in enumerate((cin, cout)):
                    m = mm(cc_ps[:, i:i + 1], t[:, :, :].rearrange("p h g -> p (h g)"), ones[0:1, 0:1],
                           start=True, stop=True)
                m.then_inc(s_ccp, 1)
                pe.wait_ge(s_fx, c + 1)
                mm(fb_ps, ones[0:1, 0:F1], fexp[:, :], start=True, stop=True).then_inc(s_fb, 1)
                pe.wait_ge(s_mx, c + 1)
                for j in range(EPP):
                    m = mm(M_ps.rearrange("p (r j) -> p r j", j=EPP)[:, :, j], view(mx[:, :], [[EPP, P]], j),
                           ident[0:R2, 0:R2], start=True, stop=True)
                m.then_inc(s_M, 1)
                pe.wait_ge(s_ohp, c + 1)
                for g in range(CG):
                    if g % 8 == 0 and c:
                        pe.wait_ge(s_acc, 2 * (c - 1) + g // 8 + 1)
                    for j in range(EPP):
                        t = g * EPP + j
                        m = mm(po[g // 8][0:F, (g % 8) * H * WIN:(g % 8 + 1) * H * WIN], edge[c % 3][:, t, :],
                               scaled[:, t, :, :].rearrange("p h w -> p (h w)"), start=(j == 0), stop=(j == EPP - 1))
                    if g % 8 == 7:
                        for j in range(EPP):
                            m = mm(po[g // 8][F:F1, :], ones[:, 0:1],
                                   view(scaled[:, (g - 7) * EPP + j, 0, :], [[EPP * H * WIN, 8], [1, H * WIN]]),
                                   start=(j == 0), stop=(j == EPP - 1))
                        m.then_inc(s_o, 1)
            pe.wait_ge(s_acc, 2 * NCH)
            zbank = [pt[0], pt[1], po[0], po[1]]
            for i in range(NZ):
                if i >= 4:
                    pe.wait_ge(s_zv, i - 3)
                for b in range(i * ZB, min(NB, (i + 1) * ZB)):
                    for hd in range(H):
                        w0 = ((b % ZB) * H + hd) * F1
                        m = mm(zbank[i % 4][0:NP_, w0:w0 + F1],
                               bass.AP(acc[:, :, :].tensor, acc[0:F1, hd, b:b + 1].offset, [list(acc[0:F1, hd, 0:1].ap[0]), [NB, NP_]]),
                               wz[:, hd, :], start=True, stop=True)
                m.then_inc(s_z, 1)
            for i in range(2):
                pe.wait_ge(s_bn, 1 + 2 * i)
                mm(p_s[:, 0:F], ones[0:NP_, :], st[0:NP_, 2 * i, :], start=True, stop=True).then_inc(s_bp, 1)

        @block.vector
        def _(dve):
            v = nc.vector
            done = [0]

            def step(ins, *also):
                done[0] += 1
                ins.then_inc(s_v, 1)
                dve.wait_ge(s_v, done[0])

            def signal(s):
                dve.sem_inc(s, 1)

            step(v.memset(srow_i[0:RP, RG - 1, :], 0))
            signal(s_pz)
            step(v.memset(ones[:, :], 1.0))
            step(v.memset(zrow[:, :], 0.0))
            step(v.memset(wl2[:, :], 0.0))
            step(v.memset(quarter, 0.0))
            for r in range(4):
                step(v.memset(view(quarter[r * WIN:(r + 1) * WIN], [[2 * EPP, RP // 2]], (r // EPP) * EPP + r % EPP), 1.0))
            step(v.memset(wz[:, :, :], 0.0))
            step(v.memset(tail_in[:, :, 0:1], -BIG))
            step(v.memset(head_in[:, :, CG:CG + 1], -BIG))
            dve.wait_ge(s_src, 48)
            step(v.tensor_copy(srow[0:RP], srow_i[0:RP]))
            signal(s_rows_f[0])
            dve.wait_ge(s_x, 32)
            step(v.tensor_reduce(ln_a[0:NP_, :], xln[0:NP_], AX.X, ALU.add))
            step(v.tensor_scalar(ln_b[0:NP_, :], ln_a[0:NP_, :], 1.0 / F, None, ALU.mult))
            step(v.tensor_tensor(tln[0:NP_], xln[0:NP_], view(ln_b[0:NP_, :], [[1, NB], [0, F]]), ALU.subtract))
            signal(s_pq)
            n_rt = 0
            for g in range(RG):
                for j in range(EPP):
                    dve.wait_ge(s_rt, n_rt + 1)
                    step(v.tensor_copy(srcI[:, g * RP:(g + 1) * RP, j], pt[n_rt % 2][:, 0:RP]))
                    signal(s_rte)
                    n_rt += 1
            signal(s_srcI)
            dve.wait_ge(s_aq, 1)
            step(v.tensor_reduce(ln_a[0:NP_, :], xln[0:NP_], AX.X, ALU.add))
            step(v.tensor_scalar(ln_a[0:NP_, :], ln_a[0:NP_, :], 1.0 / F, LN_EPS, ALU.mult, ALU.add))
            signal(s_pq)
            dve.wait_ge(s_aq, 2)
            step(v.reciprocal(ln_a[0:NP_, :], ln_b[0:NP_, :]))
            step(v.scalar_tensor_tensor(xln[0:NP_], tln[0:NP_], 0.0, view(ln_a[0:NP_, :], [[1, NB], [0, F]]),
                                        ALU.max, ALU.mult))
            signal(s_rows)
            dve.wait_ge(s_w, 96)
            for i, ab in enumerate((alb, arb)):
                step(v.tensor_tensor(wtmp[:, :], Wd[:, :], ab[:, :], ALU.mult))
                step(v.tensor_reduce(wlr[:, i * H:(i + 1) * H], wtmp[:, :].rearrange("p (h d) -> p h d", h=H), AX.X, ALU.add))
            for j in range(EPP):
                step(v.tensor_copy(wl2[j * F:(j + 1) * F, j * H:(j + 1) * H], wlr[j * F:(j + 1) * F, 0:H]))
            step(v.tensor_copy(wrB[:, :, :], view(wlr[0:F, H:2 * H], [[1, H], [0, P]])))
            signal(s_wr)
            for hd in range(H):
                step(v.tensor_copy(wz[0:F, hd, 0:F], Wd[0:F, hd * F:(hd + 1) * F]))
                step(v.memset(wz[F:F1, hd, F:F1], 1.0))
            dve.wait_ge(s_wrp, 1)
            step(v.tensor_copy(wrb[:, :, :], p_q[:, 0:H * F].rearrange("p (h f) -> p h f", h=H)))
            for hd in range(H):
                step(v.tensor_tensor(tln[0:NP_], xln[0:NP_], view(wrb[0:NP_, hd, :], [[0, NB], [1, F]]), ALU.mult))
                step(v.tensor_reduce(er[0:NP_, :, hd], tln[0:NP_], AX.X, ALU.add))
            signal(s_rows)
            dve.wait_ge(s_drw, 16)
            step(v.tensor_copy(drw[0:RP], drw_i[0:RP]))
            step(v.tensor_copy(ln_a[0:RP, 0:RG], drw[0:RP, :, 0]))
            step(v.tensor_tensor(drw[0:RP], drw[0:RP], view(ln_a[0:RP, 0:RG], [[1, RG], [0, GROUP]]), ALU.subtract))
            signal(s_rows_f[1])
            for g in range(RG):
                for j in range(EPP):
                    dve.wait_ge(s_rt, n_rt + 1)
                    step(v.tensor_copy(rel[:, g * RP:(g + 1) * RP, j], pt[n_rt % 2][:, 0:RP]))
                    signal(s_rte)
                    n_rt += 1
            dve.wait_ge(s_gp, 1)
            step(v.tensor_copy(iota[:, :], iota_i[:, :]))

            def make_e(c):
                q = c % 2
                dve.wait_ge(s_g[q], 16 * gathers_upto(c))
                dve.wait_ge(s_b[c % 3], 16 * bonds_upto(c))
                step(v.tensor_tensor(edge[c % 3], gat[q], edge[c % 3], ALU.add))
                signal(s_E)

            def make_onehot(c):
                q = c % 2
                if c >= 2:
                    dve.wait_ge(s_S, c - 1)
                step(v.tensor_tensor(onehot[:, q, :, :], view(iota[:, :], [[0, CT], [1, WIN]]),
                                     view(rel[:, c * CG, :], [[1, CT], [0, WIN]]), ALU.is_equal))
                signal(s_oh)

            make_e(0)
            make_onehot(0)
            dve.wait_ge(s_erg, 16 * RG)
            for hd in range(H):
                for r in range(4):
                    step(v.tensor_copy(view(tln_rep[0:RP], [[H * P, RG], [1, WIN]], hd * P + r * WIN),
                                       view(erg[0:RP], [[WIN * H, RG], [H, WIN]], hd)))
            signal(s_ergc)
            for g in range(RG):
                for hd in range(H):
                    dve.wait_ge(s_rt, n_rt + 1)
                    step(v.tensor_tensor(er_bd[:, g * RP:(g + 1) * RP, :, hd],
                                         view(pt[n_rt % 2][:, 0:RP], [[1, RP], [0, EPP]]), quarter, ALU.mult))
                    signal(s_rte)
                    n_rt += 1
            dve.wait_ge(s_htab, 32)
            step(v.memset(acc[0:F1, :, :], 0.0))
            dve.wait_ge(s_bases, 16)

            for c in range(NCH):
                q = c % 2
                dve.wait_ge(s_d, 32 * (c + 1))
                step(v.tensor_copy(drow[:, :], drow2_i[:, :]))
                signal(s_drc)
                step(v.tensor_tensor(pen[:, :], drow[:, 1:GROUP + 2], drow[:, 0:GROUP + 1], ALU.not_equal))
                step(v.tensor_scalar(pen[:, :], pen[:, :], -BIG, None, ALU.mult))
                own = drow[:, 1:GROUP + 1]
                step(v.tensor_scalar(pen_first[:, :], own, drow[:, 1:2], -BIG, ALU.not_equal, ALU.mult))
                step(v.tensor_scalar(pen_last[:, :], own, drow[:, GROUP:GROUP + 1], -BIG, ALU.not_equal, ALU.mult))
                step(v.tensor_scalar(rowsum[:, LINKF:LINKF + 1], drow[:, GROUP:GROUP + 1], drow[:, 0:1], -BIG,
                                     ALU.not_equal, ALU.mult))
                step(v.tensor_scalar(rowsum[:, LINKB:LINKB + 1], drow[:, 1:2], drow[:, GROUP + 1:GROUP + 2], -BIG,
                                     ALU.not_equal, ALU.mult))
                step(v.tensor_copy(rowsum[:, CONNF:CONNF + 1], pen[:, 0:1]))
                step(v.tensor_copy(rowsum[:, CONNB:CONNB + 1], pen[:, GROUP:GROUP + 1]))
                if c + 1 < NCH:
                    make_onehot(c + 1)
                dve.wait_ge(s_Sc, c + 1)
                step(v.scalar_tensor_tensor(s_lr[:, :, :, :], s_raw[:, :, :, :], NEG_SLOPE, s_raw[:, :, :, :],
                                            ALU.mult, ALU.max))
                signal(s_leaky)
                dve.wait_ge(s_sT, c + 1)
                step(v.tensor_tensor_scan(fw[:, :], pen[:, 0:GROUP], sT_ps, -BIG, ALU.add, ALU.max))
                step(v.tensor_tensor_scan(view(bw[:, :], [[-1, GROUP]], GROUP - 1),
                                          view(pen[:, :], [[-1, GROUP]], GROUP),
                                          view(sT_ps, [[-1, GROUP]], GROUP - 1), -BIG, ALU.add, ALU.max))
                step(v.tensor_copy(rowsum[:, TAILC:TAILC + 1], fw[:, GROUP - 1:GROUP]))
                step(v.tensor_copy(rowsum[:, HEADC:HEADC + 1], bw[:, 0:1]))
                signal(s_rs)
                step(v.tensor_tensor(mx[:, :], fw[:, :], bw[:, :], ALU.max))
                dve.wait_ge(s_row, c + 1)

                step(v.tensor_copy(fw[0:1, 0:6 * R2], row_ps[:, :]))
                rows = fw[0:1, 0:6 * R2]

                def rw(i, hd):
                    return fw[0:1, i * R2 + hd * CG:i * R2 + (hd + 1) * CG]

                for hd in range(H):
                    step(v.tensor_tensor_scan(tail_in[:, hd, 1:CG + 1], rw(LINKF, hd), rw(TAILC, hd),
                                              tail_in[:, hd, 0:1], ALU.add, ALU.max))
                    step(v.tensor_tensor_scan(view(head_in[:, hd, :], [[-1, CG]], CG - 1),
                                              view(rw(LINKB, hd), [[-1, CG]], CG - 1),
                                              view(rw(HEADC, hd), [[-1, CG]], CG - 1), -BIG, ALU.add, ALU.max))
                step(v.tensor_tensor(cin[:, :, :], tail_in[:, :, 0:CG],
                                     view(rows, [[CG, H], [1, CG]], CONNF * R2), ALU.add))
                step(v.tensor_tensor(cout[:, :, :], head_in[:, :, 1:CG + 1],
                                     view(rows, [[CG, H], [1, CG]], CONNB * R2), ALU.add))
                signal(s_cc)
                step(v.tensor_tensor(fmax[:, :, :], cin[:, :, 0:1], head_in[:, :, 0:1], ALU.max))
                step(v.tensor_tensor(fdif[:, :], cin[:, :, 0], fmax[:, :, 0], ALU.subtract))
                signal(s_fd)
                step(v.tensor_copy(tail_in[:, :, 0:1], tail_in[:, :, CG:CG + 1]))
                dve.wait_ge(s_ccp, c + 1)
                step(v.tensor_copy(cc[:, :], cc_ps))
                step(v.scalar_tensor_tensor(mx[:, :], pen_first[:, :], cc[:, 0:1], mx[:, :], ALU.add, ALU.max))
                step(v.scalar_tensor_tensor(mx[:, :], pen_last[:, :], cc[:, 1:2], mx[:, :], ALU.add, ALU.max))
                signal(s_mx)
                dve.wait_ge(s_M, c + 1)
                step(v.tensor_tensor(sdif[:, :, :, :].rearrange("p h g j -> p (h g j)"),
                                     s_lr[:, :, :, :].rearrange("p h g j -> p (h g j)"), M_ps, ALU.subtract))
                signal(s_sd)
                if c + 1 < NCH:
                    make_e(c + 1)
                dve.wait_ge(s_p, c + 1)
                if c:
                    dve.wait_ge(s_o, 2 * c)
                step(v.tensor_tensor(scaled[:, :, :, :], view(onehot[:, q, :, :], [[WIN, CT], [0, H], [1, WIN]]),
                                     view(p_e[:, :, :], [[1, CT], [CT, H], [0, WIN]]), ALU.mult))
                signal(s_ohp)
                base = base_regs(c)
                dve.wait_ge(s_fb, c + 1)
                at = acc[0:F1, :, bass.ds(base[0], 1)]
                step(v.tensor_tensor(at, at, fb_ps.unsqueeze(2), ALU.mult))
                for g in range(CG):
                    if g % 8 == 0:
                        dve.wait_ge(s_o, 2 * c + g // 8 + 1)
                    at = acc[0:F1, :, bass.ds(base[g], WIN)]
                    w0 = (g % 8) * H * WIN
                    step(v.tensor_tensor(at, at, po[g // 8][0:F1, w0:w0 + H * WIN].rearrange("p (h w) -> p h w", h=H),
                                         ALU.add))
                    if g % 8 == 7:
                        signal(s_acc)
            zbank = [pt[0], pt[1], po[0], po[1]]
            for i in range(NZ):
                nb = min(NB, (i + 1) * ZB) - i * ZB
                dve.wait_ge(s_z, i + 1)
                z = zbank[i % 4][0:NP_, :]
                step(v.tensor_scalar(rden[0:NP_, 0:nb, :], view(z, [[H * F1, nb], [F1, H]], F), 1e-30, float(H),
                                     ALU.max, ALU.mult))
                step(v.reciprocal(rden[0:NP_, 0:nb, :], rden[0:NP_, 0:nb, :]))
                step(v.tensor_tensor(zw[0:NP_, 0:nb, :, :], view(z, [[H * F1, nb], [F1, H], [1, F]]),
                                     view(rden[0:NP_, 0:nb, :], [[H, nb], [1, H], [0, F]]), ALU.mult))
                signal(s_zv)
                step(v.tensor_tensor(zt[0:NP_, i * ZB:i * ZB + nb, :], zw[0:NP_, 0:nb, 0, :], zw[0:NP_, 0:nb, 1, :],
                                     ALU.add))
            step(v.tensor_reduce(st[0:NP_, 0, :], zt[0:NP_].rearrange("p b f -> p f b"), AX.X, ALU.add))
            signal(s_bn)
            dve.wait_ge(s_bp, 1)
            step(v.tensor_scalar(st[:, 1, :], p_s[:, 0:F], 1.0 / N, None, ALU.mult))
            step(v.tensor_tensor(zt[0:NP_], zt[0:NP_], view(st[0:NP_, 1, :], [[0, NB], [1, F]]), ALU.subtract))
            signal(s_bn)
            dve.wait_ge(s_ba, 1)
            step(v.tensor_reduce(st[0:NP_, 2, :], tln[0:NP_].rearrange("p b f -> p f b"), AX.X, ALU.add))
            signal(s_bn)
            dve.wait_ge(s_bp, 2)
            step(v.tensor_scalar(st[:, 3, :], p_s[:, 0:F], 1.0 / N, BN_EPS, ALU.mult, ALU.add))
            signal(s_bn)
            dve.wait_ge(s_ba, 2)
            step(v.reciprocal(st[:, 5, :], st[:, 4, :]))
            step(v.tensor_tensor(st[:, 5, :], st[:, 5, :], gb[:, 0, :], ALU.mult))
            dve.wait_ge(s_xe, 32)
            for b0, b1 in QS:
                nb = b1 - b0
                zq, xq = zt[0:NP_, b0:b1], xln[0:NP_, b0:b1]
                step(v.tensor_tensor(zq, zq, view(st[0:NP_, 5, :], [[0, nb], [1, F]]), ALU.mult))
                step(v.tensor_tensor(zq, zq, view(gb[0:NP_, 1, :], [[0, nb], [1, F]]), ALU.add))
                step(v.scalar_tensor_tensor(zq, zq, 0.0, xq, ALU.max, ALU.add))
                signal(s_y)


_INS = ["x", "src", "dst", "edge_attr_64", "L0_gnn_W", "L0_gnn_attn_l", "L0_gnn_attn_r", "L0_gnn_bn_gamma",
        "L0_gnn_bn_beta"]


def kernel(**inputs):
    import numpy as _np
    import concourse.bacc as _bacc
    from concourse import mybir as _mybir
    from concourse.bass_utils import run_bass_kernel_spmd as _run

    nc = _bacc.Bacc("TRN2", target_bir_lowering=False, num_devices=1)
    arrays, args = {}, []
    for name in _INS:
        a = _np.ascontiguousarray(inputs[name])
        arrays[f"in_{name}"] = a
        args.append(nc.dram_tensor(f"in_{name}", a.shape, _mybir.dt.from_np(a.dtype), kind="ExternalInput").ap())
    args.append(nc.dram_tensor("out_0", (N, F), _mybir.dt.float32, kind="ExternalOutput").ap())
    gnn_kernel(nc, *args)
    r = _run(nc, [arrays], core_ids=[0])
    return r.results[0]["out_0"]
```

```python
import concourse.bass as bass
from concourse import mybir
from contextlib import ExitStack

N, E, F, H = 12500, 200000, 64, 2
P = 128
EPP = 2
GROUP = P * EPP
WIN = 32
CG = 16
CT = CG * EPP
CHUNK = CG * GROUP
NCH = -(-E // CHUNK)
NGR = -(-E // GROUP)
NGP = NCH * CG
RP = 112
RG = NGP // RP
assert RP * RG == NGP
FULL = E // GROUP
TAIL = E - FULL * GROUP
assert TAIL % EPP == 0 and FULL + 1 == NGR
EPAD = NGP * GROUP
NACC = N + WIN
NP_, NB = 125, 100
assert NP_ * NB == N
PS = (0, 112, 125)
EW_ROWS = 12512
F1 = F + 1
BIG = 1.0e37
NEG_SLOPE, LN_EPS, BN_EPS = 0.2, 1e-5, 1e-5
BP = 96
GT = 125
SROW = H + H * (F + 1)
assert E % GT == 0 and N % GT == 0
NR = 2
ZBL = NP_ * NR
NZ = N // ZBL
assert NZ * ZBL == N
LAG = 2
ZIN = NCH - LAG


def gnn_kernel(nc, x, src, dst, ea, W, attn_l, attn_r, gamma, beta, out):
    f32, i32 = mybir.dt.float32, mybir.dt.int32
    ALU, ACT, AX = mybir.AluOpType, mybir.ActivationFunctionType, mybir.AxisListType

    def view(ap, dims, off=0):
        return bass.AP(ap.tensor, ap.offset + off, [list(ap.ap[0])] + [list(d) for d in dims])

    with ExitStack() as ctx:
        def sb(name, shape, dt=f32):
            return ctx.enter_context(nc.sbuf_tensor(name, shape, dt))

        def sem(name):
            return ctx.enter_context(nc.semaphore(name))

        h_tab = nc.dram_tensor("h_tab", (N, F), f32, kind="Internal").ap()
        er_tab = nc.dram_tensor("er_tab", ((EW_ROWS + WIN) * H,), f32, kind="Internal").ap()
        er_win = nc.dram_tensor("er_win", (EW_ROWS, WIN * H), f32, kind="Internal").ap()
        dst_pad = nc.dram_tensor("dst_pad", (EPAD + 2,), i32, kind="Internal").ap()
        state_tab = nc.dram_tensor("state_tab", (N, SROW), f32, kind="Internal").ap()

        acc = sb("acc", [P, H, NACC])
        accf = acc[:, :, :].rearrange("p h n -> p (h n)")
        SLOT = CT * F
        work = sb("work", [P, 2 * SLOT + NZ * NR * F])
        assert NZ * NR * F >= 3 * SLOT
        gat = [view(work[:, :], [[F, CT], [1, F]], i * SLOT) for i in (0, 2)]
        edge = [view(work[:, :], [[F, CT], [1, F]], i * SLOT) for i in (1, 3, 4)]
        assert (NCH - 1) % 2 == 0 and (NCH - 1) % 3 == 0
        xres = view(work[:, :], [[NR * F, NZ], [1, NR * F]], 2 * SLOT)
        assert NR * F <= ZBL
        zt = view(accf, [[ZBL, NZ], [F, NR], [1, F]])
        onehot = sb("onehot", [P, 2, CT, WIN])
        scaled = sb("scaled", [P, CT, H, WIN])
        eT = sb("eT", [P, CG, P])
        ohT = sb("ohT", [P, CG // 2, P])
        srcI = sb("srcI", [P, NGP, EPP], i32)
        rel = sb("rel", [P, NGP, EPP])
        er_bd = sb("er_bd", [P, NGP, EPP, H])
        ident = sb("ident", [P, P])
        ones = sb("ones", [P, P])
        iota_i = sb("iota_i", [P, WIN], i32)
        iota = sb("iota", [P, WIN])
        neg1 = sb("neg1", [1, 1], i32)
        zero1 = sb("zero1", [P, 1])
        wlr = sb("wlr", [P, 2 * H])
        wl2 = sb("wl2", [P, EPP * H])
        wb = sb("wb", [P, 2 * H, F])
        flag = sb("flag", [P, 1], i32)[BP:BP + 1]
        flag_n = sb("flag_n", [P, 2])[BP:BP + 1]
        wz = sb("wz", [F1, H, F1])
        gb = sb("gb", [P, 2, F])
        R2 = H * CG
        s_raw = sb("s_raw", [P, H, CG, EPP])
        s_lr = sb("s_lr", [P, H, CG, EPP])
        sdif = sb("sdif", [P, H, CG, EPP])
        p_e = sb("p_e", [P, H, CT])
        drow2_i = sb("drow2_i", [R2, GROUP + 2], i32)
        drow = sb("drow", [R2, GROUP + 2])
        pen = sb("pen", [R2, GROUP + 1])
        pen_first = sb("pen_first", [R2, GROUP])
        pen_last = sb("pen_last", [R2, GROUP])
        fw = sb("fw", [R2, GROUP])
        bw = sb("bw", [R2, GROUP])
        mx = sb("mx", [R2, GROUP])
        rowsum = sb("rowsum", [R2, 6])
        tail_in = sb("tail_in", [1, H, CG + 1])
        head_in = sb("head_in", [1, H, CG + 1])
        cin = sb("cin", [1, H, CG])
        cout = sb("cout", [1, H, CG])
        cc = sb("cc", [R2, 2])
        fmax = sb("fmax", [1, H, 1])
        fdif = sb("fdif", [1, H])
        fexp = sb("fexp", [1, H])
        rden = sb("rden", [P, NR, H])
        zw = sb("zw", [P, NR, H, F])
        zd = sb("zd", [P, NR, F])
        zmean = sb("zmean", [P, NR, F])
        zdev = sb("zdev", [P, NR, F])
        TAILC, HEADC, CONNF, LINKF, CONNB, LINKB = range(6)

        xln = view(accf, [[F, NB], [1, F]])
        tln = view(accf, [[F, NB], [1, F]], NB * F)
        o = 2 * NB * F
        srow_i = view(accf, [[GROUP, RG], [1, GROUP]], o).bitcast(i32)
        srow = view(accf, [[GROUP, RG], [1, GROUP]], o + RG * GROUP)
        GW = GROUP + 1
        drw_i = view(accf, [[GW, RG], [1, GW]], o + 2 * RG * GROUP).bitcast(i32)
        drw = view(accf, [[GW, RG], [1, GW]], o + 2 * RG * GROUP + RG * GW)
        erg = view(accf, [[WIN * H, RG], [1, WIN * H]], o + 2 * RG * GROUP + 2 * RG * GW)
        taken = [o + 2 * RG * GROUP + 2 * RG * GW + RG * WIN * H]

        def lend(*dims):
            size = 1
            for d in dims:
                size *= d
            taken[0] += size
            assert taken[0] <= H * NACC
            step_, ap = size, []
            for d in dims:
                step_ //= d
                ap.append([step_, d])
            return view(accf, ap, taken[0] - size)

        padc = lend(EPAD + 1 - E)[0:1].bitcast(i32)
        zrow = lend((EW_ROWS + WIN - N) * H)[0:1]
        Wd, alb, arb, wtmp = (lend(H * F) for _ in range(4))
        wB = lend(2 * H, P)[0:F]
        odd = srow[0:RP]
        odd_n = lend(2)
        ln_a, ln_b, ln_m, er = lend(NB), lend(NB), lend(NB), lend(NB, H)
        quarter = lend(RP, EPP)
        st = view(scaled[:, 0, 0, :], [[F, 6], [1, F]])
        due = lend(3, NCH - LAG)[BP:BP + 1]
        due_all = lend(NCH - LAG).bitcast(i32)
        due_i = due_all[BP:BP + 1]
        bases = lend(NGP)[BP:BP + 1].bitcast(i32)

        given = [0]

        def piece(*dims):
            size = 1
            for d in dims:
                size *= d
            given[0] += size
            assert given[0] <= 2 * SLOT
            step_, ap = size, []
            for d in dims:
                step_ //= d
                ap.append([step_, d])
            return view(work[:, :], ap, given[0] - size)[0:GT]

        g_src, g_dst, g_to, g_row_i = (piece(n).bitcast(i32) for n in (1, 1, 1, GT))
        g_row, g_same, g_apart, g_below, g_tmp = (piece(GT) for _ in range(5))
        g_dstf, g_dup, g_h, g_ea, g_er = piece(1), piece(1), piece(F), piece(F), piece(H)
        g_e, g_prod, g_s, g_diag, g_sb = piece(F1), piece(F), piece(H), piece(H, GT), piece(H, GT)
        g_mx, g_dif, g_ex, g_u = piece(H), piece(2 * H), piece(2 * H), piece(H, F1)
        g_old, g_new, g_init = piece(SROW), piece(SROW), piece(SROW)

        pt = [ctx.enter_context(nc.psum_tensor(f"pt{i}", [P, 512], f32)) for i in range(2)]
        p_s = ctx.enter_context(nc.psum_tensor("p_s", [P, 512], f32))
        p_m = ctx.enter_context(nc.psum_tensor("p_m", [P, 512], f32))
        p_r = ctx.enter_context(nc.psum_tensor("p_r", [P, 512], f32))
        p_q = ctx.enter_context(nc.psum_tensor("p_q", [P, 512], f32))
        po = [ctx.enter_context(nc.psum_tensor(f"po{i}", [P, 512], f32)) for i in range(2)]
        S_ps = p_s[:, 0:CT * H]
        M_ps = p_m[:, 0:CT * H]
        sT_ps = p_r[0:R2, 0:GROUP]
        row_ps = p_r[0:1, GROUP:GROUP + 6 * R2]
        cc_ps = p_r[0:R2, GROUP + 6 * R2:GROUP + 6 * R2 + 2]
        fb_ps = p_m[0:F1, 256:256 + H]

        QS = [(0, 25), (25, 50), (50, 75), (75, 100)]
        OUT = [(0, 10), (10, 20), (20, 30), (30, 40), (40, 50)]
        POOL_OUT = 3
        s_xq = [sem(f"s_x{i}") for i in range(len(QS))]
        s_sub, s_subp, s_sq, s_var, s_std = sem("s_sub"), sem("s_subp"), sem("s_sq"), sem("s_var"), sem("s_std")
        s_mean, s_er, s_clear, s_zero, s_dmy = sem("s_mean"), sem("s_er"), sem("s_clear"), sem("s_zero"), sem("s_dmy")
        s_ga, s_pa, r_z, r_zv, r_v = sem("s_ga"), sem("s_pa"), sem("r_z"), sem("r_zv"), sem("r_v")
        s_src, s_w, s_dpad, s_drw = sem("s_src"), sem("s_w"), sem("s_dpad"), sem("s_drw")
        s_const, s_pz, s_gp = sem("s_const"), sem("s_pz"), sem("s_gp")
        s_bases, s_htab, s_ertab, s_erwin, s_erg = sem("s_bases"), sem("s_htab"), sem("s_ertab"), sem("s_erwin"), sem("s_erg")
        s_rows, s_rt, s_srcI = sem("s_rows"), sem("s_rt"), sem("s_srcI")
        s_v = sem("s_v")
        s_b = [sem(f"s_b{i}") for i in range(3)]
        s_d = sem("s_d")
        s_g = [sem("s_g0"), sem("s_g1")]
        s_E, s_oh, s_tr, s_te, s_S, s_Sc = sem("s_E"), sem("s_oh"), sem("s_tr"), sem("s_te"), sem("s_S"), sem("s_Sc")
        s_drc, s_leaky, s_sT, s_rs, s_row, s_cc, s_ccp = (sem("s_drc"), sem("s_leaky"), sem("s_sT"), sem("s_rs"), sem("s_row"),
                                                       sem("s_cc"), sem("s_ccp"))
        s_fd, s_fx, s_fb, s_mx, s_M, s_sd, s_p = (sem("s_fd"), sem("s_fx"), sem("s_fb"), sem("s_mx"), sem("s_M"),
                                                  sem("s_sd"), sem("s_p"))
        s_ohp, s_o, s_acc = sem("s_ohp"), sem("s_o"), sem("s_acc")
        s_z, s_zv, s_bn, s_bp, s_ba, s_xe, s_y, s_out = (sem("s_z"), sem("s_zv"), sem("s_bn"), sem("s_bp"), sem("s_ba"),
                                                         sem("s_xe"), sem("s_y"), sem("s_out"))

        s_rows_f = [sem("s_rows_src"), sem("s_rows_dst")]
        s_rte, s_wr, s_wrp, s_ergc = sem("s_rte"), sem("s_wr"), sem("s_wrp"), sem("s_ergc")
        s_odd, s_oddp, s_flag = sem("s_odd"), sem("s_oddp"), sem("s_flag")
        tln_rep = view(accf, [[1, RG * H * P]], NB * F)

        def base_regs(c):
            return nc.values_load_multi_w_load_instructions(
                bases[0:1, c * CG:(c + 1) * CG], engines=[mybir.EngineType.DVE], min_val=0, max_val=N)[1]

        def groups_in(c):
            return min(CG, NGR - c * CG)

        def gathers_upto(c):
            return sum(EPP * groups_in(i) for i in range(c % 2, c + 1, 2))

        def bond_dmas(c):
            return 2 if (c + 1) * CHUNK > E else 1

        def bonds_upto(c):
            return sum(bond_dmas(i) for i in range(c % 3, c + 1, 3))

        RB = 512 // (RP * EPP)
        BATCH = [(g, min(RG, g + RB)) for g in range(0, RG, RB)]
        NRT = len(BATCH)

        def columns(t, g0, g1):
            return view(t[:, g0 * RP, :], [[RP * EPP, g1 - g0], [1, EPP], [EPP, RP]])

        def bank_rows(n, sets):
            return pt[n % 2][:, 0:sets * EPP * RP].rearrange("p (g j k) -> p g j k", j=EPP, k=RP)
        q_init, q_src, q_dst, q_row, q_ea = sem("q_init"), sem("q_src"), sem("q_dst"), sem("q_row"), sem("q_ea")
        q_h, q_er, q_old, q_to, q_free = sem("q_h"), sem("q_er"), sem("q_old"), sem("q_to"), sem("q_free")
        q_diag, q_bc, q_dif, q_ex, q_u, q_sum, q_new = (sem("q_diag"), sem("q_bc"), sem("q_dif"), sem("q_ex"),
                                                        sem("q_u"), sem("q_sum"), sem("q_new"))
        q_c, q_rl, q_rt, q_rc, q_done = sem("q_c"), sem("q_rl"), sem("q_rt"), sem("q_rc"), sem("q_done")

        def if_flag(eng, which):
            eng.wait_ge(s_flag, 1)
            r = nc.values_load(flag, engines=[which], min_val=0, max_val=1)
            return eng.If(r != 0)

        def z_bank(b):
            return p_q if b < ZIN else (p_q, pt[0], pt[1])[b % 3]

        ENG = mybir.EngineType

        block = ctx.enter_context(nc.Block())

        @block.sync
        def _(sp):
            sp.wait_ge(s_pz, 1)
            fullg = FULL // RP
            rest = FULL - fullg * RP
            sp.dma_start(srow_i[0:RP, 0:fullg, :],
                         src[0:fullg * RP * GROUP].rearrange("(g p e) -> p g e", p=RP, e=GROUP)).then_inc(s_src, 16)
            sp.dma_start(srow_i[0:rest, fullg, :],
                         src[fullg * RP * GROUP:FULL * GROUP].rearrange("(p e) -> p e", e=GROUP)).then_inc(s_src, 16)
            sp.dma_start(srow_i[rest:rest + 1, fullg, 0:TAIL],
                         src[FULL * GROUP:E].rearrange("(p e) -> p e", p=1)).then_inc(s_src, 16)
            sp.dma_start(dst_pad[1:1 + E].rearrange("(a b) -> a b", a=16),
                         dst[0:E].rearrange("(a b) -> a b", a=16)).then_inc(s_dpad, 16)
            sp.wait_ge(s_gp, 1)
            sp.dma_start(dst_pad[1 + E:EPAD + 2].rearrange("(p e) -> p e", p=1), padc[:, :]).then_inc(s_dpad, 16)
            sp.dma_start(dst_pad[0:1].rearrange("(p e) -> p e", p=1), neg1[:, :]).then_inc(s_dpad, 16)
            sp.wait_ge(s_dpad, 48)
            sp.dma_start(drw_i[0:RP], bass.AP(dst_pad.tensor, 1, [[GROUP, RP], [RP * GROUP, RG], [1, GW]])).then_inc(s_drw, 16)
            with nc.allow_non_contiguous_dma(reason="first dst of each group"):
                sp.dma_start(bases[:, :], bass.AP(dst_pad.tensor, 1, [[1, 1], [GROUP, NGP], [1, 1]])).then_inc(s_bases, 16)

            def load_chunk(c):
                q = c % 3
                if c >= 3:
                    sp.wait_ge(s_o, 2 * (c - 2))
                ng = min(CG, FULL - c * CG)
                sp.dma_start(edge[q].rearrange("p (g j) f -> p g (j f)", j=EPP)[:, 0:ng, :],
                             ea[c * CHUNK:c * CHUNK + ng * GROUP, :].rearrange("(g p j) f -> p g (j f)", p=P, j=EPP)
                             ).then_inc(s_b[q], 16)
                if bond_dmas(c) == 2:
                    sp.dma_start(edge[q].rearrange("p (g j) f -> p g (j f)", j=EPP)[0:TAIL // EPP, ng, :],
                                 ea[FULL * GROUP:E, :].rearrange("(p j) f -> p (j f)", j=EPP)).then_inc(s_b[q], 16)
                if c >= 1:
                    sp.wait_ge(s_drc, c)
                for hd in range(H):
                    sp.dma_start(drow2_i[hd * CG:(hd + 1) * CG, :],
                                 bass.AP(dst_pad.tensor, c * CHUNK, [[GROUP, CG], [1, GROUP + 2]])).then_inc(s_d, 16)

            load_chunk(0)
            for i, (b0, b1) in enumerate(QS):
                sp.wait_ge(s_rows, i + 1)
                for p0, p1 in zip(PS, PS[1:]):
                    sp.dma_start(h_tab.rearrange("(p b) f -> p b f", b=NB)[p0:p1, b0:b1], xln[p0:p1, b0:b1]
                                 ).then_inc(s_htab, 16)
            sp.wait_ge(s_er, 1)
            for p0, p1 in zip(PS, PS[1:]):
                sp.dma_start(er_tab[0:N * H].rearrange("(p b) -> p b", b=NB * H)[p0:p1],
                             er[p0:p1].rearrange("p b h -> p (b h)")).then_inc(s_ertab, 16)
            sp.dma_start(er_tab[N * H:(EW_ROWS + WIN) * H].rearrange("(p e) -> p e", p=1), zrow[:, :]).then_inc(s_ertab, 16)
            sp.wait_ge(s_ertab, 48)
            sp.dma_start(er_win[:, :], bass.AP(er_tab.tensor, 0, [[H, EW_ROWS], [1, WIN * H]])).then_inc(s_erwin, 16)
            for c in range(1, NCH):
                load_chunk(c)
            sp.wait_ge(s_o, 2 * (NCH - 1))
            for p0, p1 in zip(PS, PS[1:]):
                sp.dma_start(xres[p0:p1], x.rearrange("(b p r) f -> p b (r f)", p=NP_, r=NR)[p0:p1]).then_inc(s_xe, 16)
            sp.wait_ge(s_acc, 2 * NCH)
            with if_flag(sp, ENG.SP):
                sp.wait_ge(q_init, 1)
                sp.dma_start(state_tab.rearrange("(p b) c -> p b c", p=GT), view(g_init, [[0, N // GT], [1, SROW]])
                             ).then_inc(q_c, 16)
                with sp.Fori(0, E // GT) as i:
                    sp.wait_ge(q_free, i + 1)
                    for t, sm, a in ((g_src, q_src, src), (g_dst, q_dst, dst)):
                        sp.dma_start(t, a[bass.ds(i * GT, GT)].rearrange("(p o) -> p o", o=1)).then_inc(sm, 16)
                    row = dst[bass.ds(i * GT, GT)]
                    sp.dma_start(g_row_i, row.rearrange("(o e) -> o e", o=1).broadcast_to([GT, GT])).then_inc(q_row, 16)
                    sp.dma_start(g_ea, ea[bass.ds(i * GT, GT), :]).then_inc(q_ea, 16)
                sp.wait_ge(q_free, E // GT + 1)
                with sp.Fori(0, N // GT) as b:
                    sp.wait_ge(q_rt, b + 1)
                    sp.dma_start(g_old, state_tab[bass.ds(b * GT, GT), :]).then_inc(q_rl, 16)
            for i, (b0, b1) in enumerate(OUT):
                sp.wait_ge(s_y, i + 1)
                for p0, p1 in zip(PS, PS[1:]):
                    sp.dma_start(out.rearrange("(b p r) f -> p b (r f)", p=NP_, r=NR)[p0:p1, b0:b1],
                                 zt[p0:p1, b0:b1].rearrange("p b r f -> p b (r f)")).then_inc(s_out, 16)
            sp.wait_ge(s_htab, 32 * len(QS))
            sp.wait_ge(s_erwin, 16)
            sp.wait_ge(s_out, 32 * len(OUT))

        @block.gpsimd
        def _(pool):
            nc.gpsimd.memset(padc[:, :], N).then_inc(s_const, 1)
            nc.gpsimd.memset(neg1[:, :], -1).then_inc(s_const, 1)
            nc.gpsimd.memset(ident[:, :], 0.0).then_inc(s_const, 1)
            nc.gpsimd.iota(iota_i[:, :], [[1, WIN]], base=0, channel_multiplier=0).then_inc(s_const, 1)
            pool.wait_ge(s_const, 4)
            nc.gpsimd.affine_select(out=ident[:, :], in_=ident[:, :], compare_op=ALU.not_equal, fill=1.0, base=0,
                                    pattern=[[-1, P]], channel_multiplier=1).then_inc(s_gp, 1)
            nc.gpsimd.iota(due_all, [[ZBL, NCH - LAG]], base=ZBL, channel_multiplier=0).then_inc(s_const, 1)
            for i, (b0, b1) in enumerate(QS):
                if i:
                    pool.wait_ge(s_mean, i + 1)
                    nc.gpsimd.tensor_tensor(tln[0:NP_, b0:b1], xln[0:NP_, b0:b1],
                                            view(ln_m[0:NP_, b0:b1], [[1, b1 - b0], [0, F]]), ALU.subtract
                                            ).then_inc(s_subp, 1)

            def gather(c):
                q = c % 2
                if c >= 2:
                    pool.wait_ge(s_E, c - 1)
                for g in range(groups_in(c)):
                    for j in range(EPP):
                        k = c * CG + g
                        pool.indirect_dma_start(out=gat[q][:, g * EPP + j, :], out_offset=None, in_=h_tab,
                                                in_offset=bass.IndirectOffsetOnAxis(ap=srcI[:, k, j:j + 1], axis=0)
                                                ).then_inc(s_g[q], 16)

            pool.wait_ge(s_srcI, NRT)
            pool.wait_ge(s_htab, 32 * len(QS))
            gather(0)
            gather(1)
            pool.wait_ge(s_erwin, 16)
            pool.wait_ge(s_drw, 16)
            for g in range(RG):
                pool.indirect_dma_start(out=erg[0:RP, g, :], out_offset=None, in_=er_win,
                                        in_offset=bass.IndirectOffsetOnAxis(ap=drw_i[0:RP, g, 0:1], axis=0)
                                        ).then_inc(s_erg, 16)
            for c in range(2, NCH):
                gather(c)
            pool.wait_ge(s_acc, 2 * NCH)
            with if_flag(pool, ENG.Pool):
                def wait_for(producer, count):
                    pool.wait_ge(producer, count)
                    pool.sem_clear(producer)

                at = bass.IndirectOffsetOnAxis
                pool.wait_ge(q_init, 1)
                nc.gpsimd.affine_select(out=g_below, in_=ones[0:GT, 0:GT], compare_op=ALU.is_gt, fill=0.0, base=0,
                                        pattern=[[-1, GT]], channel_multiplier=1).then_inc(q_free, 1)
                pool.wait_ge(q_c, 16)
                with pool.Fori(0, E // GT) as i:
                    wait_for(q_src, 16)
                    pool.indirect_dma_start(out=g_h, out_offset=None, in_=h_tab,
                                            in_offset=at(ap=g_src, axis=0)).then_inc(q_h, 16)
                    wait_for(q_dst, 16)
                    pool.indirect_dma_start(out=g_er, out_offset=None, in_=er_tab.rearrange("(n h) -> n h", h=H),
                                            in_offset=at(ap=g_dst, axis=0)).then_inc(q_er, 16)
                    pool.indirect_dma_start(out=g_old, out_offset=None, in_=state_tab,
                                            in_offset=at(ap=g_dst, axis=0)).then_inc(q_old, 16)
                    wait_for(q_new, 1)
                    pool.indirect_dma_start(out=state_tab, out_offset=at(ap=g_to, axis=0), in_=g_new, in_offset=None,
                                            bounds_check=N - 1, oob_is_err=False).then_inc(q_to, 16)
                    pool.wait_ge(q_to, i * 16 + 16)
                    pool.sem_inc(q_free, 1)
            pool.wait_ge(s_ga, 1)
            for i, (b0, b1) in enumerate(OUT):
                if i >= POOL_OUT:
                    zq = zt[0:NP_, b0:b1]
                    for k, op in ((0, ALU.mult), (1, ALU.add)):
                        nc.gpsimd.tensor_tensor(zq, zq, view(st[0:NP_, k, :], [[0, b1 - b0], [0, NR], [1, F]]), op
                                                ).then_inc(s_pa, 1)
                        pool.wait_ge(s_pa, 2 * (i - POOL_OUT) + k + 1)

        @block.scalar
        def _(act):
            for i, (b0, b1) in enumerate(QS):
                for p0, p1 in zip(PS, PS[1:]):
                    act.dma_start(xln[p0:p1, b0:b1], x.rearrange("(p b) f -> p b f", b=NB)[p0:p1, b0:b1]
                                  ).then_inc(s_xq[i], 16)
            for a in range(2):
                act.dma_start(Wd[a * F:(a + 1) * F, :], W[:, :]).then_inc(s_w, 16)
            for t, v in ((alb[:, :], attn_l), (arb[:, :], attn_r)):
                act.dma_start(t, bass.AP(v.tensor, 0, [[0, P], [1, H * F]])).then_inc(s_w, 16)
            for i, v in enumerate((gamma, beta)):
                act.dma_start(gb[:, i, :], bass.AP(v.tensor, 0, [[0, P], [1, F]])).then_inc(s_w, 16)
            def square(i):
                b0, b1 = QS[i]
                if i == 0:
                    act.wait_ge(s_sub, 1)
                else:
                    act.wait_ge(s_subp, i)
                nc.scalar.activation(xln[0:NP_, b0:b1], tln[0:NP_, b0:b1], ACT.Square).then_inc(s_sq, 1)

            def root(i):
                b0, b1 = QS[i]
                act.wait_ge(s_var, i + 1)
                nc.scalar.activation(ln_b[0:NP_, b0:b1], ln_a[0:NP_, b0:b1], ACT.Sqrt).then_inc(s_std, 1)

            act.wait_ge(s_src, 48)
            nc.scalar.activation(srow[0:RP], srow_i[0:RP], ACT.Copy).then_inc(s_rows_f[0], 1)
            square(0)
            for n, (g0, g1) in enumerate(BATCH):
                act.wait_ge(s_rt, n + 1)
                nc.scalar.activation(columns(srcI, g0, g1), bank_rows(n, g1 - g0), ACT.Copy).then_inc(s_srcI, 1)
            for i in range(1, len(QS)):
                square(i)
                root(i - 1)
            root(len(QS) - 1)
            act.wait_ge(s_clear, 1)
            nc.scalar.activation(acc[0:F1, 1, :], view(zero1[0:F1, :], [[0, NACC]]), ACT.Copy).then_inc(s_zero, 1)

            n_tr = 0
            for c in range(NCH):
                for r in range(6):
                    n_tr += 1
                    act.wait_ge(s_tr, n_tr)
                    if r == 0 and c:
                        act.wait_ge(s_S, c)
                    dest = eT[:, 4 * r:4 * r + 4, :] if r < 4 else ohT[:, 4 * (r - 4):4 * (r - 4) + 4, :]
                    nc.scalar.activation(dest, pt[(n_tr - 1) % 2][:, :].rearrange("p (a b) -> p a b", b=P), ACT.Copy
                                         ).then_inc(s_te, 1)
                act.wait_ge(s_S, c + 1)
                if c:
                    act.wait_ge(s_leaky, c)
                nc.scalar.activation(s_raw[:, :, :, :].rearrange("p h g j -> p g j h"),
                                     S_ps.rearrange("p (g j h) -> p g j h", j=EPP, h=H), ACT.Copy).then_inc(s_Sc, 1)
                act.wait_ge(s_fd, c + 1)
                if c:
                    act.wait_ge(s_fb, c)
                nc.scalar.activation(fexp[:, :], fdif[:, :], ACT.Exp).then_inc(s_fx, 1)
                act.wait_ge(s_sd, c + 1)
                if c:
                    act.wait_ge(s_ohp, c)
                nc.scalar.activation(p_e[:, :, :], sdif[:, :, :, :].rearrange("p h g j -> p h (g j)"), ACT.Exp
                                     ).then_inc(s_p, 1)
            with if_flag(act, ENG.Activation):
                with act.Fori(0, E // GT) as i:
                    act.wait_ge(q_dif, i + 1)
                    nc.scalar.activation(g_ex, g_dif, ACT.Exp).then_inc(q_ex, 1)
            nc.scalar.activation(fexp[:, 0:1], ones[0:1, 0:1], ACT.Sqrt).then_inc(s_dmy, 1)
            act.wait_ge(s_bn, 3)
            nc.scalar.activation(st[:, 4, :], st[:, 3, :], ACT.Sqrt).then_inc(s_ba, 1)

        @block.tensor
        def _(pe):
            mm = nc.tensor.matmul
            def z_block(b, made, read):
                bank = z_bank(b)
                if bank is p_q and b:
                    pe.wait_ge(read, min(b, ZIN))
                for r in range(NR):
                    for hd in range(H):
                        c0 = (r * H + hd) * F1
                        m = mm(bank[0:NP_, c0:c0 + F1], view(acc[0:F1, hd, 0:1], [[NR, NP_]], b * ZBL + r),
                               wz[:, hd, :], start=True, stop=True)
                m.then_inc(made, 1)

            def copied_out(n):
                pe.wait_ge(s_srcI if n <= NRT else s_rte, n if n <= NRT else n - NRT)

            pe.wait_ge(s_gp, 1)
            n_rt = 0
            for arr, ready in ((srow, s_rows_f[0]), (drw, s_rows_f[1])):
                if arr is drw:
                    pe.wait_ge(s_wr, 1)
                    for i in range(2 * H):
                        m = mm(p_q[:, i * F:(i + 1) * F], wB[:, i, :], ident[0:F, 0:F], start=True, stop=True)
                    m.then_inc(s_wrp, 1)
                pe.wait_ge(ready, 1)
                for g0, g1 in BATCH:
                    if n_rt >= 2:
                        copied_out(n_rt - 1)
                    for g in range(g0, g1):
                        for j in range(EPP):
                            m = mm(bank_rows(n_rt, g1 - g0)[:, g - g0, j, :],
                                   view(arr[0:RP], [[EPP, P]], g * (GW if arr is drw else GROUP) + j),
                                   ident[0:RP, 0:RP], start=True, stop=True)
                    m.then_inc(s_rt, 1)
                    n_rt += 1
            pe.wait_ge(s_odd, 1)
            mm(p_s[:, 0:1], ones[0:RP, :], odd_n[0:RP, 0:1], start=True, stop=True).then_inc(s_oddp, 1)
            pe.wait_ge(s_ergc, 1)
            for g in range(RG):
                copied_out(n_rt - 1)
                for hd in range(H):
                    m = mm(pt[n_rt % 2][:, hd * RP:(hd + 1) * RP], tln_rep[0:RP, (g * H + hd) * P:(g * H + hd + 1) * P],
                           ident[0:RP, 0:RP], start=True, stop=True)
                m.then_inc(s_rt, 1)
                n_rt += 1
            copied_out(n_rt)

            n_tr = 0
            for c in range(NCH):
                q = c % 2
                pe.wait_ge(s_E, c + 1)
                for r in range(6):
                    if r == 4:
                        pe.wait_ge(s_oh, c + 1)
                    if n_tr >= 2:
                        pe.wait_ge(s_te, n_tr - 1)
                    for i in range(4):
                        if r < 4:
                            t0 = (4 * r + i) * EPP
                            a = edge[c % 3][:, t0:t0 + EPP, :].rearrange("p t f -> p (t f)")
                        else:
                            t0 = (4 * (r - 4) + i) * 4
                            a = onehot[:, q, t0:t0 + 4, :].rearrange("p t w -> p (t w)")
                        m = nc.tensor.transpose(pt[n_tr % 2][:, i * P:(i + 1) * P], a, ident[:, :])
                    m.then_inc(s_tr, 1)
                    n_tr += 1
                pe.wait_ge(s_te, n_tr)
                if c:
                    pe.wait_ge(s_Sc, c)
                for g in range(CG):
                    k = c * CG + g
                    if g % 2 == 0:
                        mm(S_ps[:, g * 4:g * 4 + 8], ohT[:, g // 2, :],
                           er_bd[:, k:k + 2, :, :].rearrange("p k j h -> p (k j h)"),
                           start=True, stop=False, skip_group_check=True)
                    m = mm(S_ps[:, g * 4:g * 4 + 4], eT[:, g, :], wl2[:, :], start=False, stop=True,
                           skip_group_check=True)
                m.then_inc(s_S, 1)
                if c >= LAG:
                    pe.wait_ge(s_acc, 2 * c)
                    z_block(c - LAG, s_z, s_zv)
                pe.wait_ge(s_leaky, c + 1)
                for j in range(EPP):
                    m = mm(view(sT_ps, [[EPP, P]], j), s_lr[:, :, :, j].rearrange("p h g -> p (h g)"), ident[:, :],
                           start=True, stop=True)
                m.then_inc(s_sT, 1)
                pe.wait_ge(s_rs, c + 1)
                for i in range(6):
                    m = mm(row_ps[:, i * R2:(i + 1) * R2], rowsum[:, i:i + 1], ident[0:R2, 0:R2], start=True, stop=True)
                m.then_inc(s_row, 1)
                pe.wait_ge(s_cc, c + 1)
                for i, t in enumerate((cin, cout)):
                    m = mm(cc_ps[:, i:i + 1], t[:, :, :].rearrange("p h g -> p (h g)"), ones[0:1, 0:1],
                           start=True, stop=True)
                m.then_inc(s_ccp, 1)
                pe.wait_ge(s_fx, c + 1)
                mm(fb_ps, ones[0:1, 0:F1], fexp[:, :], start=True, stop=True).then_inc(s_fb, 1)
                pe.wait_ge(s_mx, c + 1)
                for j in range(EPP):
                    m = mm(M_ps.rearrange("p (r j) -> p r j", j=EPP)[:, :, j], view(mx[:, :], [[EPP, P]], j),
                           ident[0:R2, 0:R2], start=True, stop=True)
                m.then_inc(s_M, 1)
                pe.wait_ge(s_ohp, c + 1)
                for g in range(CG):
                    if g % 8 == 0 and c:
                        pe.wait_ge(s_acc, 2 * (c - 1) + g // 8 + 1)
                    for j in range(EPP):
                        t = g * EPP + j
                        m = mm(po[g // 8][0:F, (g % 8) * H * WIN:(g % 8 + 1) * H * WIN], edge[c % 3][:, t, :],
                               scaled[:, t, :, :].rearrange("p h w -> p (h w)"), start=(j == 0), stop=(j == EPP - 1))
                    if g % 8 == 7:
                        for j in range(EPP):
                            m = mm(po[g // 8][F:F1, :], ones[:, 0:1],
                                   view(scaled[:, (g - 7) * EPP + j, 0, :], [[EPP * H * WIN, 8], [1, H * WIN]]),
                                   start=(j == 0), stop=(j == EPP - 1))
                        m.then_inc(s_o, 1)
            pe.wait_ge(s_acc, 2 * NCH)
            for b in range(ZIN, NZ):
                z_block(b, s_z, s_zv)
            with if_flag(pe, ENG.PE):
                with pe.Fori(0, E // GT) as i:
                    pe.wait_ge(q_diag, i + 1)
                    mm(p_s[0:GT, 0:H * GT], ones[0:GT, 0:GT], g_diag.rearrange("p h e -> p (h e)"),
                       start=True, stop=True).then_inc(q_bc, 1)
                    pe.wait_ge(q_u, i + 1)
                    mm(p_m[0:GT, 0:H * F1], g_same, g_u.rearrange("p h f -> p (h f)"),
                       start=True, stop=True).then_inc(q_sum, 1)
                pe.sem_inc(q_rt, 1)
                with pe.Fori(0, N // GT) as b:
                    pe.wait_ge(q_rl, b * 16 + 16)
                    pe.wait_ge(q_rc, b + 1)
                    for hd in range(H):
                        m = mm(p_r[0:F1, hd * GT:(hd + 1) * GT], g_old[:, H + hd * F1:H + (hd + 1) * F1],
                               ident[0:GT, 0:GT], start=True, stop=True)
                    m.then_inc(q_rt, 1)
                pe.wait_ge(q_done, 1)
                for b in range(NZ):
                    if b:
                        pe.wait_ge(r_zv, b)
                    z_block(b, r_z, r_zv)
            for i, t in enumerate((zmean, zdev)):
                pe.wait_ge(s_bn, 1 + i)
                mm(p_s[:, 0:NR * F], ones[0:NP_, :], t[0:NP_, :, :].rearrange("p r f -> p (r f)"),
                   start=True, stop=True).then_inc(s_bp, 1)

        @block.vector
        def _(dve):
            v = nc.vector
            done = [s_v, 0]

            def step(ins):
                done[1] += 1
                ins.then_inc(done[0], 1)
                dve.wait_ge(done[0], done[1])

            def signal(s):
                dve.sem_inc(s, 1)

            step(v.memset(srow_i[0:RP, RG - 1, :], 0))
            signal(s_pz)
            step(v.memset(ones[:, :], 1.0))
            step(v.memset(zero1[:, :], 0.0))
            step(v.memset(zrow[:, :], 0.0))
            step(v.memset(wl2[:, :], 0.0))
            step(v.memset(quarter, 0.0))
            for r in range(4):
                step(v.memset(view(quarter[r * WIN:(r + 1) * WIN], [[2 * EPP, RP // 2]], (r // EPP) * EPP + r % EPP), 1.0))
            step(v.memset(wz[:, :, :], 0.0))
            step(v.memset(tail_in[:, :, 0:1], -BIG))
            step(v.memset(head_in[:, :, CG:CG + 1], -BIG))
            def mean(i):
                b0, b1 = QS[i]
                dve.wait_ge(s_xq[i], 32)
                step(v.tensor_reduce(ln_a[0:NP_, b0:b1], xln[0:NP_, b0:b1], AX.X, ALU.add))
                step(v.tensor_scalar(ln_m[0:NP_, b0:b1], ln_a[0:NP_, b0:b1], 1.0 / F, None, ALU.mult))
                signal(s_mean)

            def variance(i):
                b0, b1 = QS[i]
                dve.wait_ge(s_sq, i + 1)
                step(v.tensor_reduce(ln_a[0:NP_, b0:b1], xln[0:NP_, b0:b1], AX.X, ALU.add))
                step(v.tensor_scalar(ln_a[0:NP_, b0:b1], ln_a[0:NP_, b0:b1], 1.0 / F, LN_EPS, ALU.mult, ALU.add))
                signal(s_var)

            def normed(i):
                b0, b1 = QS[i]
                dve.wait_ge(s_std, i + 1)
                step(v.reciprocal(ln_a[0:NP_, b0:b1], ln_b[0:NP_, b0:b1]))
                step(v.scalar_tensor_tensor(xln[0:NP_, b0:b1], tln[0:NP_, b0:b1], 0.0,
                                            view(ln_a[0:NP_, b0:b1], [[1, b1 - b0], [0, F]]), ALU.max, ALU.mult))
                signal(s_rows)

            mean(0)
            b0, b1 = QS[0]
            step(v.tensor_tensor(tln[0:NP_, b0:b1], xln[0:NP_, b0:b1],
                                 view(ln_m[0:NP_, b0:b1], [[1, b1 - b0], [0, F]]), ALU.subtract))
            signal(s_sub)
            mean(1)
            variance(0)
            mean(2)
            normed(0)
            mean(3)
            for i in range(1, len(QS)):
                variance(i)
                if i > 1:
                    normed(i - 1)
            normed(len(QS) - 1)
            dve.wait_ge(s_w, 96)
            for i, ab in enumerate((alb, arb)):
                step(v.tensor_tensor(wtmp[:, :], Wd[:, :], ab[:, :], ALU.mult))
                step(v.tensor_reduce(wlr[:, i * H:(i + 1) * H], wtmp[:, :].rearrange("p (h d) -> p h d", h=H), AX.X, ALU.add))
            for j in range(EPP):
                step(v.tensor_copy(wl2[j * F:(j + 1) * F, j * H:(j + 1) * H], wlr[j * F:(j + 1) * F, 0:H]))
            step(v.tensor_copy(wB[:, :, :], view(wlr[0:F, :], [[1, 2 * H], [0, P]])))
            signal(s_wr)
            for hd in range(H):
                step(v.tensor_copy(wz[0:F, hd, 0:F], Wd[0:F, hd * F:(hd + 1) * F]))
                step(v.memset(wz[F:F1, hd, F:F1], 1.0))
            dve.wait_ge(s_wrp, 1)
            step(v.tensor_copy(wb[:, :, :], p_q[:, 0:2 * H * F].rearrange("p (i f) -> p i f", f=F)))
            for hd in range(H):
                step(v.tensor_tensor(tln[0:NP_], xln[0:NP_], view(wb[0:NP_, H + hd, :], [[0, NB], [1, F]]), ALU.mult))
                step(v.tensor_reduce(er[0:NP_, :, hd], tln[0:NP_], AX.X, ALU.add))
            signal(s_er)
            n_rt = NRT
            dve.wait_ge(s_drw, 16)
            step(v.tensor_copy(drw[0:RP], drw_i[0:RP]))
            step(v.tensor_copy(ln_a[0:RP, 0:RG], drw[0:RP, :, 0]))
            step(v.tensor_tensor(drw[0:RP], drw[0:RP], view(ln_a[0:RP, 0:RG], [[1, RG], [0, GW]]), ALU.subtract))
            signal(s_rows_f[1])
            for g0, g1 in BATCH:
                dve.wait_ge(s_rt, n_rt + 1)
                step(v.tensor_copy(columns(rel, g0, g1), bank_rows(n_rt, g1 - g0)))
                signal(s_rte)
                n_rt += 1
            dve.wait_ge(s_gp, 1)
            step(v.tensor_copy(iota[:, :], iota_i[:, :]))

            def make_e(c):
                q = c % 2
                dve.wait_ge(s_g[q], 16 * gathers_upto(c))
                dve.wait_ge(s_b[c % 3], 16 * bonds_upto(c))
                step(v.tensor_tensor(edge[c % 3], gat[q], edge[c % 3], ALU.add))
                signal(s_E)

            def make_onehot(c):
                q = c % 2
                if c >= 2:
                    dve.wait_ge(s_S, c - 1)
                step(v.tensor_tensor(onehot[:, q, :, :], view(iota[:, :], [[0, CT], [1, WIN]]),
                                     view(rel[:, c * CG, :], [[1, CT], [0, WIN]]), ALU.is_equal))
                signal(s_oh)

            make_e(0)
            make_onehot(0)
            step(v.tensor_tensor(odd, drw[0:RP, :, 1:GW], drw[0:RP, :, 0:GROUP], ALU.is_lt))
            step(v.tensor_reduce(odd_n[0:RP, 0:1], odd, AX.XY, ALU.add))
            step(v.tensor_scalar(odd, drw[0:RP, :, 0:GROUP], float(WIN), None, ALU.is_ge))
            step(v.tensor_reduce(odd_n[0:RP, 1:2], odd, AX.XY, ALU.add))
            step(v.tensor_tensor(odd_n[0:RP, 0:1], odd_n[0:RP, 0:1], odd_n[0:RP, 1:2], ALU.add))
            signal(s_odd)
            dve.wait_ge(s_oddp, 1)
            step(v.tensor_scalar(flag_n[:, 0:1], p_s[BP:BP + 1, 0:1], 0.0, None, ALU.is_gt))
            dve.wait_ge(s_bases, 16)
            dve.wait_ge(s_const, 5)
            step(v.tensor_copy(due[:, 0, :], view(bases, [[CG, NCH - LAG]], LAG * CG)))
            step(v.tensor_copy(due[:, 1, :], due_i))
            step(v.tensor_tensor(due[:, 2, :], due[:, 0, :], due[:, 1, :], ALU.is_lt))
            step(v.tensor_reduce(flag_n[:, 1:2], due[:, 2, :], AX.X, ALU.max))
            step(v.tensor_tensor(flag, flag_n[:, 0:1], flag_n[:, 1:2], ALU.max))
            step(v.tensor_scalar(flag_n[:, 0:1], flag, float(N), None, ALU.mult))
            step(v.tensor_scalar(bases, bases, flag_n[:, 0:1], None, ALU.max))
            signal(s_flag)
            make_e(1)
            dve.wait_ge(s_erg, 16 * RG)
            for hd in range(H):
                for r in range(4):
                    step(v.tensor_copy(view(tln_rep[0:RP], [[H * P, RG], [1, WIN]], hd * P + r * WIN),
                                       view(erg[0:RP], [[WIN * H, RG], [H, WIN]], hd)))
            signal(s_ergc)
            for g in range(RG):
                dve.wait_ge(s_rt, n_rt + 1)
                step(v.tensor_tensor(view(er_bd[:, g * RP, 0, :], [[1, H], [EPP * H, RP], [H, EPP]]),
                                     view(pt[n_rt % 2][:, :], [[RP, H], [1, RP], [0, EPP]]),
                                     view(quarter, [[0, H], [EPP, RP], [1, EPP]]), ALU.mult))
                signal(s_rte)
                n_rt += 1
            dve.wait_ge(s_htab, 32 * len(QS))
            dve.wait_ge(s_ertab, 48)
            signal(s_clear)
            step(v.memset(acc[0:F1, 0, :], 0.0))
            step(v.memset(zmean[:, :, :], 0.0))
            step(v.memset(zdev[:, :, :], 0.0))

            def z_block(b, made, read):
                z = z_bank(b)[0:NP_, :]
                n, zb, d = zw[0:NP_], zt[0:NP_, b], zd[0:NP_]
                dve.wait_ge(made, b + 1)
                step(v.tensor_scalar(rden[0:NP_], view(z, [[H * F1, NR], [F1, H]], F), 1e-30, float(H), ALU.max, ALU.mult))
                step(v.reciprocal(rden[0:NP_], rden[0:NP_]))
                step(v.tensor_tensor(n, view(z, [[H * F1, NR], [F1, H], [1, F]]),
                                     view(rden[0:NP_, 0, :], [[H, NR], [1, H], [0, F]]), ALU.mult))
                signal(read)
                step(v.tensor_tensor(zb, n[:, :, 0, :], n[:, :, 1, :], ALU.add))
                step(v.tensor_tensor(d, zb, zmean[0:NP_], ALU.subtract))
                step(v.scalar_tensor_tensor(zmean[0:NP_], d, 1.0 / (b + 1), zmean[0:NP_], ALU.mult, ALU.add))
                step(v.tensor_tensor(n[:, :, 0, :], zb, zmean[0:NP_], ALU.subtract))
                step(v.tensor_tensor(d, d, n[:, :, 0, :], ALU.mult))
                step(v.tensor_tensor(zdev[0:NP_], zdev[0:NP_], d, ALU.add))


            for c in range(NCH):
                q = c % 2
                dve.wait_ge(s_d, 32 * (c + 1))
                step(v.tensor_copy(drow[:, :], drow2_i[:, :]))
                signal(s_drc)
                step(v.tensor_tensor(pen[:, :], drow[:, 1:GROUP + 2], drow[:, 0:GROUP + 1], ALU.not_equal))
                step(v.tensor_scalar(pen[:, :], pen[:, :], -BIG, None, ALU.mult))
                own = drow[:, 1:GROUP + 1]
                step(v.tensor_scalar(pen_first[:, :], own, drow[:, 1:2], -BIG, ALU.not_equal, ALU.mult))
                step(v.tensor_scalar(pen_last[:, :], own, drow[:, GROUP:GROUP + 1], -BIG, ALU.not_equal, ALU.mult))
                step(v.tensor_scalar(rowsum[:, LINKF:LINKF + 1], drow[:, GROUP:GROUP + 1], drow[:, 0:1], -BIG,
                                     ALU.not_equal, ALU.mult))
                step(v.tensor_scalar(rowsum[:, LINKB:LINKB + 1], drow[:, 1:2], drow[:, GROUP + 1:GROUP + 2], -BIG,
                                     ALU.not_equal, ALU.mult))
                step(v.tensor_copy(rowsum[:, CONNF:CONNF + 1], pen[:, 0:1]))
                step(v.tensor_copy(rowsum[:, CONNB:CONNB + 1], pen[:, GROUP:GROUP + 1]))
                if c + 1 < NCH:
                    make_onehot(c + 1)
                dve.wait_ge(s_Sc, c + 1)
                step(v.scalar_tensor_tensor(s_lr[:, :, :, :], s_raw[:, :, :, :], NEG_SLOPE, s_raw[:, :, :, :],
                                            ALU.mult, ALU.max))
                signal(s_leaky)
                dve.wait_ge(s_sT, c + 1)
                step(v.tensor_tensor_scan(fw[:, :], pen[:, 0:GROUP], sT_ps, -BIG, ALU.add, ALU.max))
                step(v.tensor_tensor_scan(view(bw[:, :], [[-1, GROUP]], GROUP - 1),
                                          view(pen[:, :], [[-1, GROUP]], GROUP),
                                          view(sT_ps, [[-1, GROUP]], GROUP - 1), -BIG, ALU.add, ALU.max))
                step(v.tensor_copy(rowsum[:, TAILC:TAILC + 1], fw[:, GROUP - 1:GROUP]))
                step(v.tensor_copy(rowsum[:, HEADC:HEADC + 1], bw[:, 0:1]))
                signal(s_rs)
                step(v.tensor_tensor(mx[:, :], fw[:, :], bw[:, :], ALU.max))
                dve.wait_ge(s_row, c + 1)

                step(v.tensor_copy(fw[0:1, 0:6 * R2], row_ps[:, :]))
                rows = fw[0:1, 0:6 * R2]

                def rw(i, hd):
                    return fw[0:1, i * R2 + hd * CG:i * R2 + (hd + 1) * CG]

                for hd in range(H):
                    step(v.tensor_tensor_scan(tail_in[:, hd, 1:CG + 1], rw(LINKF, hd), rw(TAILC, hd),
                                              tail_in[:, hd, 0:1], ALU.add, ALU.max))
                    step(v.tensor_tensor_scan(view(head_in[:, hd, :], [[-1, CG]], CG - 1),
                                              view(rw(LINKB, hd), [[-1, CG]], CG - 1),
                                              view(rw(HEADC, hd), [[-1, CG]], CG - 1), -BIG, ALU.add, ALU.max))
                step(v.tensor_tensor(cin[:, :, :], tail_in[:, :, 0:CG],
                                     view(rows, [[CG, H], [1, CG]], CONNF * R2), ALU.add))
                step(v.tensor_tensor(cout[:, :, :], head_in[:, :, 1:CG + 1],
                                     view(rows, [[CG, H], [1, CG]], CONNB * R2), ALU.add))
                signal(s_cc)
                step(v.tensor_tensor(fmax[:, :, :], cin[:, :, 0:1], head_in[:, :, 0:1], ALU.max))
                step(v.tensor_tensor(fdif[:, :], cin[:, :, 0], fmax[:, :, 0], ALU.subtract))
                signal(s_fd)
                step(v.tensor_copy(tail_in[:, :, 0:1], tail_in[:, :, CG:CG + 1]))
                dve.wait_ge(s_ccp, c + 1)
                step(v.tensor_copy(cc[:, :], cc_ps))
                step(v.scalar_tensor_tensor(mx[:, :], pen_first[:, :], cc[:, 0:1], mx[:, :], ALU.add, ALU.max))
                step(v.scalar_tensor_tensor(mx[:, :], pen_last[:, :], cc[:, 1:2], mx[:, :], ALU.add, ALU.max))
                signal(s_mx)
                dve.wait_ge(s_M, c + 1)
                step(v.tensor_tensor(sdif[:, :, :, :].rearrange("p h g j -> p (h g j)"),
                                     s_lr[:, :, :, :].rearrange("p h g j -> p (h g j)"), M_ps, ALU.subtract))
                signal(s_sd)
                dve.wait_ge(s_p, c + 1)
                if c:
                    dve.wait_ge(s_o, 2 * c)
                step(v.tensor_tensor(scaled[:, :, :, :], view(onehot[:, q, :, :], [[WIN, CT], [0, H], [1, WIN]]),
                                     view(p_e[:, :, :], [[1, CT], [CT, H], [0, WIN]]), ALU.mult))
                signal(s_ohp)
                if 1 <= c < NCH - 1:
                    make_e(c + 1)
                base = base_regs(c)
                if c == 0:
                    dve.wait_ge(s_zero, 1)
                dve.wait_ge(s_fb, c + 1)
                at = acc[0:F1, :, bass.ds(base[0], 1)]
                step(v.tensor_tensor(at, at, fb_ps.unsqueeze(2), ALU.mult))
                for g in range(CG):
                    if g % 8 == 0:
                        dve.wait_ge(s_o, 2 * c + g // 8 + 1)
                    at = acc[0:F1, :, bass.ds(base[g], WIN)]
                    w0 = (g % 8) * H * WIN
                    step(v.tensor_tensor(at, at, po[g // 8][0:F1, w0:w0 + H * WIN].rearrange("p (h w) -> p h w", h=H),
                                         ALU.add))
                    if g % 8 == 7:
                        signal(s_acc)
                if c >= LAG:
                    z_block(c - LAG, s_z, s_zv)
            for b in range(ZIN, NZ):
                z_block(b, s_z, s_zv)
            with if_flag(dve, ENG.DVE):
                def run(*ins):
                    dve.drain()

                run(v.memset(g_init[:, 0:H], -BIG))
                run(v.memset(g_init[:, H:SROW], 0.0))
                run(v.memset(g_e[:, F:F1], 1.0))
                signal(q_init)
                with dve.Fori(0, E // GT) as i:
                    dve.wait_ge(q_row, i * 16 + 16)
                    dve.wait_ge(q_old, i * 16 + 16)
                    run(v.tensor_copy(g_dstf, g_dst))
                    run(v.tensor_copy(g_row, g_row_i))
                    run(v.tensor_scalar(g_same, g_row, g_dstf, None, ALU.is_equal))
                    run(v.tensor_scalar(g_apart, g_row, g_dstf, -BIG, ALU.not_equal, ALU.mult))
                    dve.wait_ge(q_free, i + 1)
                    run(v.tensor_tensor(g_tmp, g_same, g_below, ALU.mult))
                    run(v.tensor_reduce(g_dup, g_tmp, AX.X, ALU.max))
                    run(v.scalar_tensor_tensor(g_to, g_dup, float(N), g_dstf, ALU.mult, ALU.add))
                    dve.wait_ge(q_h, i * 16 + 16)
                    dve.wait_ge(q_ea, i * 16 + 16)
                    run(v.tensor_tensor(g_e[:, 0:F], g_h, g_ea, ALU.add))
                    for hd in range(H):
                        run(v.tensor_tensor(g_prod, g_e[:, 0:F], wb[0:GT, hd, :], ALU.mult))
                        run(v.tensor_reduce(g_s[:, hd:hd + 1], g_prod, AX.X, ALU.add))
                    dve.wait_ge(q_er, i * 16 + 16)
                    run(v.tensor_tensor(g_s, g_s, g_er, ALU.add))
                    run(v.scalar_tensor_tensor(g_s, g_s, NEG_SLOPE, g_s, ALU.mult, ALU.max))
                    for hd in range(H):
                        run(v.tensor_scalar(g_diag[:, hd, :], ident[0:GT, 0:GT], g_s[:, hd:hd + 1], None, ALU.mult))
                    signal(q_diag)
                    dve.wait_ge(q_bc, i + 1)
                    run(v.tensor_tensor(g_sb, p_s[0:GT, 0:H * GT].rearrange("p (h e) -> p h e", h=H),
                                        view(g_apart, [[0, H], [1, GT]]), ALU.add))
                    run(v.tensor_reduce(g_mx, g_sb, AX.X, ALU.max))
                    dve.wait_ge(q_old, i * 16 + 16)
                    run(v.tensor_tensor(g_mx, g_mx, g_old[:, 0:H], ALU.max))
                    run(v.tensor_tensor(g_dif[:, 0:H], g_s, g_mx, ALU.subtract))
                    run(v.tensor_tensor(g_dif[:, H:2 * H], g_old[:, 0:H], g_mx, ALU.subtract))
                    signal(q_dif)
                    dve.wait_ge(q_ex, i + 1)
                    for hd in range(H):
                        run(v.tensor_scalar(g_u[:, hd, :], g_e, g_ex[:, hd:hd + 1], None, ALU.mult))
                    signal(q_u)
                    run(v.tensor_copy(g_new[:, 0:H], g_mx))
                    dve.wait_ge(q_sum, i + 1)
                    for hd in range(H):
                        c0 = H + hd * F1
                        run(v.scalar_tensor_tensor(g_new[:, c0:c0 + F1], g_old[:, c0:c0 + F1], g_ex[:, H + hd:H + hd + 1],
                                                   p_m[0:GT, hd * F1:(hd + 1) * F1], ALU.mult, ALU.add))
                    signal(q_new)
                signal(q_rc)
                with dve.Fori(0, N // GT) as b:
                    dve.wait_ge(q_rt, b + 2)
                    run(v.tensor_copy(acc[0:F1, :, bass.ds(b * GT, GT)],
                                      p_r[0:F1, 0:H * GT].rearrange("p (h n) -> p h n", h=H)))
                    signal(q_rc)
                signal(q_done)
                usual, done[:] = list(done), [r_v, 0]
                step(v.memset(zmean[:, :, :], 0.0))
                step(v.memset(zdev[:, :, :], 0.0))
                for b in range(NZ):
                    z_block(b, r_z, r_zv)
                done[:] = usual
            signal(s_bn)
            mu, dm = st[:, 2, :], zd[0:NP_]
            dve.wait_ge(s_bp, 1)
            step(v.tensor_reduce(mu, p_s[:, 0:NR * F].rearrange("p (r f) -> p f r", r=NR), AX.X, ALU.add))
            step(v.tensor_scalar(mu, mu, 1.0 / ZBL, None, ALU.mult))
            step(v.tensor_tensor(dm, zmean[0:NP_], view(mu[0:NP_], [[0, NR], [1, F]]), ALU.subtract))
            step(v.tensor_tensor(dm, dm, dm, ALU.mult))
            step(v.scalar_tensor_tensor(zdev[0:NP_], dm, float(NZ), zdev[0:NP_], ALU.mult, ALU.add))
            signal(s_bn)
            dve.wait_ge(s_bp, 2)
            step(v.tensor_reduce(st[:, 3, :], p_s[:, 0:NR * F].rearrange("p (r f) -> p f r", r=NR), AX.X, ALU.add))
            step(v.tensor_scalar(st[:, 3, :], st[:, 3, :], 1.0 / N, BN_EPS, ALU.mult, ALU.add))
            signal(s_bn)
            dve.wait_ge(s_ba, 1)
            step(v.reciprocal(st[:, 5, :], st[:, 4, :]))
            step(v.tensor_tensor(st[:, 0, :], st[:, 5, :], gb[:, 0, :], ALU.mult))
            step(v.tensor_tensor(st[:, 5, :], mu, st[:, 0, :], ALU.mult))
            step(v.tensor_tensor(st[:, 1, :], gb[:, 1, :], st[:, 5, :], ALU.subtract))
            signal(s_ga)
            dve.wait_ge(s_xe, 32)
            for i, (b0, b1) in enumerate(OUT):
                zq = zt[0:NP_, b0:b1]
                xq = xres[0:NP_, b0:b1].rearrange("p b (r f) -> p b r f", f=F)
                if i < POOL_OUT:
                    for k, op in ((0, ALU.mult), (1, ALU.add)):
                        step(v.tensor_tensor(zq, zq, view(st[0:NP_, k, :], [[0, b1 - b0], [0, NR], [1, F]]), op))
                else:
                    dve.wait_ge(s_pa, 2 * (i - POOL_OUT + 1))
                step(v.scalar_tensor_tensor(zq, zq, 0.0, xq, ALU.max, ALU.add))
                signal(s_y)


_INS = ["x", "src", "dst", "edge_attr_64", "L0_gnn_W", "L0_gnn_attn_l", "L0_gnn_attn_r", "L0_gnn_bn_gamma",
        "L0_gnn_bn_beta"]


def kernel(**inputs):
    import numpy as _np
    import concourse.bacc as _bacc
    from concourse import mybir as _mybir
    from concourse.bass_utils import run_bass_kernel_spmd as _run

    nc = _bacc.Bacc("TRN2", target_bir_lowering=False, num_devices=1)
    arrays, args = {}, []
    for name in _INS:
        a = _np.ascontiguousarray(inputs[name])
        arrays[f"in_{name}"] = a
        args.append(nc.dram_tensor(f"in_{name}", a.shape, _mybir.dt.from_np(a.dtype), kind="ExternalInput").ap())
    args.append(nc.dram_tensor("out_0", (N, F), _mybir.dt.float32, kind="ExternalOutput").ap())
    gnn_kernel(nc, *args)
    r = _run(nc, [arrays], core_ids=[0])
    return r.results[0]["out_0"]
```

```python
import concourse.bass as bass
from concourse import mybir
from contextlib import ExitStack

N, E, F, H = 12500, 200000, 64, 2
P = 128
EPP = 2
GROUP = P * EPP
WIN = 32
CG = 16
CT = CG * EPP
NQ = 4
GQ, TQ = CG // NQ, CT // NQ
AHEAD = 8
RAW = 2
CHUNK = CG * GROUP
NCH = -(-E // CHUNK)
NGR = -(-E // GROUP)
NGP = NCH * CG
RP = 112
RG = NGP // RP
assert RP * RG == NGP
FULL = E // GROUP
TAIL = E - FULL * GROUP
assert TAIL % EPP == 0 and FULL + 1 == NGR
EPAD = NGP * GROUP
NACC = N + WIN
NP_, NB = 125, 100
assert NP_ * NB == N
PS = (0, 112, 125)
EW_ROWS = 12512
F1 = F + 1
BIG = 1.0e37
NEG_SLOPE, LN_EPS, BN_EPS = 0.2, 1e-5, 1e-5
BP = 96
GT = 125
SROW = H + H * (F + 1)
assert E % GT == 0 and N % GT == 0
NR = 2
ZBL = NP_ * NR
NZ = N // ZBL
assert NZ * ZBL == N
LAG = 2
ZIN = NZ - 1


def z_upto(c):
    return max(0, min(c - LAG + 1 + 2 * (c == NCH - 1), ZIN))


def gnn_kernel(nc, x, src, dst, ea, W, attn_l, attn_r, gamma, beta, out):
    f32, i32 = mybir.dt.float32, mybir.dt.int32
    ALU, ACT, AX = mybir.AluOpType, mybir.ActivationFunctionType, mybir.AxisListType

    def view(ap, dims, off=0):
        return bass.AP(ap.tensor, ap.offset + off, [list(ap.ap[0])] + [list(d) for d in dims])

    with ExitStack() as ctx:
        def sb(name, shape, dt=f32):
            return ctx.enter_context(nc.sbuf_tensor(name, shape, dt))

        def sem(name):
            return ctx.enter_context(nc.semaphore(name))

        h_tab = nc.dram_tensor("h_tab", (N, F), f32, kind="Internal").ap()
        er_tab = nc.dram_tensor("er_tab", ((EW_ROWS + WIN) * H,), f32, kind="Internal").ap()
        er_win = nc.dram_tensor("er_win", (EW_ROWS, WIN * H), f32, kind="Internal").ap()
        dst_pad = nc.dram_tensor("dst_pad", (EPAD + 2,), i32, kind="Internal").ap()
        state_tab = nc.dram_tensor("state_tab", (N, SROW), f32, kind="Internal").ap()

        acc = sb("acc", [P, H, NACC])
        accf = acc[:, :, :].rearrange("p h n -> p (h n)")
        SLOT = CT * F
        work = sb("work", [P, 2 * SLOT + NZ * NR * F])
        assert NZ * NR * F >= 3 * SLOT
        gat = [view(work[:, :], [[F, CT], [1, F]], i * SLOT) for i in (0, 2)]
        edge = [view(work[:, :], [[F, CT], [1, F]], i * SLOT) for i in (1, 3, 4)]
        assert (NCH - 1) % 2 == 0 and (NCH - 1) % 3 == 0
        xres = view(work[:, :], [[NR * F, NZ], [1, NR * F]], 2 * SLOT)
        zT = view(accf, [[ZBL, NZ], [1, NP_]])
        onehot = sb("onehot", [P, 2, CT, WIN])
        scaled = sb("scaled", [P, CT, H, WIN])
        eT = sb("eT", [P, CG, P])
        ohT = sb("ohT", [P, CG // 2, P])
        srcI = sb("srcI", [P, NGP, EPP], i32)
        rel = sb("rel", [P, NGP, EPP])
        er_bd = sb("er_bd", [P, NGP, EPP, H])
        ident = sb("ident", [P, P])
        ones = sb("ones", [P, P])
        iota_i = sb("iota_i", [P, WIN], i32)
        iota = sb("iota", [P, WIN])
        neg1 = sb("neg1", [1, 1], i32)
        zero1 = sb("zero1", [P, 1])
        wlr = sb("wlr", [P, 2 * H])
        wl2 = sb("wl2", [P, EPP * H])
        wr2 = sb("wr2", [P, EPP * H])
        wb = sb("wb", [P, H, F])
        flag = sb("flag", [P, 1], i32)[BP:BP + 1]
        flag_n = sb("flag_n", [P, 2])[BP:BP + 1]
        wz = sb("wz", [F1, H, F1])
        gb = sb("gb", [P, 2])
        R2 = H * CG
        s_raw = sb("s_raw", [P, H, CG, EPP])
        s_lr = sb("s_lr", [P, H, CG, EPP])
        sdif = sb("sdif", [P, H, CG, EPP])
        p_e = sb("p_e", [P, H, CT])
        drow2_i = sb("drow2_i", [R2, GROUP + 2], i32)
        drow = sb("drow", [R2, GROUP + 2])
        pen = sb("pen", [R2, GROUP + 1])
        pen_first = sb("pen_first", [R2, GROUP])
        pen_last = sb("pen_last", [R2, GROUP])
        fw = sb("fw", [R2, GROUP])
        bw = sb("bw", [R2, GROUP])
        mx = sb("mx", [R2, GROUP])
        link = sb("link", [R2, 2])
        row_ends = (fw[:, GROUP - 1:GROUP], bw[:, 0:1], pen[:, 0:1], link[:, 0:1], pen[:, GROUP:GROUP + 1], link[:, 1:2])
        tail_in = sb("tail_in", [1, H, CG + 1])
        head_in = sb("head_in", [1, H, CG + 1])
        cin = sb("cin", [1, H, CG])
        cout = sb("cout", [1, H, CG])
        cc = sb("cc", [R2, 2])
        fmax = sb("fmax", [1, H, 1])
        fdif = sb("fdif", [1, H])
        fexp = sb("fexp", [1, H])
        rden = sb("rden", [P, NR, H])
        zw = sb("zw", [P, NR, H, F])
        zd = sb("zd", [P, NR, F])
        zn = sb("zn", [P, 2, NR, F])
        zz = sb("zz", [P, NR, F])
        col = sb("col", [P, 6])
        MU, VAR, STD, REC, SCALE, SHIFT = (slice(i, i + 1) for i in range(6))
        zmean = sb("zmean", [P, NR, F])
        zdev = sb("zdev", [P, NR, F])
        TAILC, HEADC, CONNF, LINKF, CONNB, LINKB = range(6)

        xln = view(accf, [[F, NB], [1, F]])
        tln = view(accf, [[F, NB], [1, F]], NB * F)
        o = 2 * NB * F
        srow_i = view(accf, [[GROUP, RG], [1, GROUP]], o).bitcast(i32)
        srow = view(accf, [[GROUP, RG], [1, GROUP]], o + RG * GROUP)
        GW = GROUP + 1
        drw_i = view(accf, [[GW, RG], [1, GW]], o + 2 * RG * GROUP).bitcast(i32)
        drw = view(accf, [[GW, RG], [1, GW]], o + 2 * RG * GROUP + RG * GW)
        erg = view(accf, [[WIN * H, RG], [1, WIN * H]], o + 2 * RG * GROUP + 2 * RG * GW)
        taken = [o + 2 * RG * GROUP + 2 * RG * GW + RG * WIN * H]

        def lend(*dims):
            size = 1
            for d in dims:
                size *= d
            taken[0] += size
            assert taken[0] <= H * NACC
            step_, ap = size, []
            for d in dims:
                step_ //= d
                ap.append([step_, d])
            return view(accf, ap, taken[0] - size)

        padc = lend(EPAD + 1 - E)[0:1].bitcast(i32)
        zrow = lend((EW_ROWS + WIN - N) * H)[0:1]
        Wd, alb, arb, wtmp = (lend(H * F) for _ in range(4))
        wB = lend(H, P)[0:F]
        odd = srow[0:RP]
        odd_n = lend(2)
        ln_a, ln_b, ln_m, er = lend(NB), lend(NB), lend(NB), lend(NB, H)
        quarter = lend(RP, EPP)
        g_mean, g_var = lend(CT), lend(CT)
        g_sq = view(accf, [[F, CT], [1, F]], NB * F + RG * H * P)
        assert RG * H * P + CT * F <= NB * F
        mu = scaled[:, 0, :, :].rearrange("p h w -> p (h w)")
        due = lend(3, NCH - LAG)[BP:BP + 1]
        due_all = lend(NCH - LAG).bitcast(i32)
        due_i = due_all[BP:BP + 1]
        bases = lend(NGP)[BP:BP + 1].bitcast(i32)

        sq0, rows1 = NB * F + RG * H * P, o + 2 * RG * GROUP
        CLEAR = [(taken[0], H * NACC), (0, NB * F), (sq0, rows1), (NB * F, sq0), (rows1, taken[0])]

        given = [0]

        def piece(*dims):
            size = 1
            for d in dims:
                size *= d
            given[0] += size
            assert given[0] <= 2 * SLOT
            step_, ap = size, []
            for d in dims:
                step_ //= d
                ap.append([step_, d])
            return view(work[:, :], ap, given[0] - size)[0:GT]

        g_src, g_dst, g_to, g_row_i = (piece(n).bitcast(i32) for n in (1, 1, 1, GT))
        g_row, g_same, g_apart, g_below, g_tmp = (piece(GT) for _ in range(5))
        g_dstf, g_dup, g_h, g_ea, g_er = piece(1), piece(1), piece(F), piece(F), piece(H)
        g_e, g_prod, g_s, g_diag, g_sb = piece(F1), piece(F), piece(H), piece(H, GT), piece(H, GT)
        g_mx, g_dif, g_ex, g_u = piece(H), piece(2 * H), piece(2 * H), piece(H, F1)
        g_old, g_new, g_init = piece(SROW), piece(SROW), piece(SROW)

        pt = [ctx.enter_context(nc.psum_tensor(f"pt{i}", [P, 512], f32)) for i in range(2)]
        p_s = ctx.enter_context(nc.psum_tensor("p_s", [P, 512], f32))
        p_m = ctx.enter_context(nc.psum_tensor("p_m", [P, 512], f32))
        p_r = ctx.enter_context(nc.psum_tensor("p_r", [P, 512], f32))
        p_q = ctx.enter_context(nc.psum_tensor("p_q", [P, 512], f32))
        po = [ctx.enter_context(nc.psum_tensor(f"po{i}", [P, 512], f32)) for i in range(2)]
        S_ps = p_s[:, 0:CT * H]
        M_ps = p_m[:, 0:CT * H]
        sT_ps = p_r[0:R2, 0:GROUP]
        row_ps = p_r[0:1, GROUP:GROUP + 6 * R2]
        cc_ps = p_r[0:R2, GROUP + 6 * R2:GROUP + 6 * R2 + 2]
        out_banks = [pt[0], pt[1], p_m, p_r, p_q, po[0], po[1]]
        fb_ps = p_m[0:F1, 256:256 + H]

        QS = [(0, 24), (24, 48), (48, 72), (72, 100)]
        TURN = [(b, min(b + 4, NZ)) for b in range(0, NZ, 4)]
        AFF = [(0, 4), (4, 8), (8, 16), (16, 24), (24, 36), (36, NZ)]
        OUT = [(0, 16), (16, 32), (32, 44), (44, NZ)]
        x_in = [sem(f"x_in{i}") for i in range(len(QS))]
        w_in = sem("w_in")
        src0_in = sem("src0_in")
        src_in = sem("src_in")
        dpad_in = sem("dpad_in")
        drw_in = sem("drw_in")
        bases_in = sem("bases_in")
        ea_in = [sem(f"ea_in{i}") for i in range(3)]
        drow_in = sem("drow_in")
        gat_in = [[sem(f"gat_in{q}_{k}") for k in range(NQ)] for q in range(2)]
        htab_in = sem("htab_in")
        ertab_in = sem("ertab_in")
        erwin_in = sem("erwin_in")
        erg_in = sem("erg_in")
        xres_in = sem("xres_in")
        out_in = sem("out_in")
        const_ok = sem("const_ok")
        ident_ok = sem("ident_ok")
        pad_zeroed = sem("pad_zeroed")
        ln_centred = sem("ln_centred")
        ln_squared = sem("ln_squared")
        ln_var = sem("ln_var")
        ln_root = sem("ln_root")
        h_ok = sem("h_ok")
        wr_ok = sem("wr_ok")
        wl_turned = sem("wl_turned")
        src0_rows = sem("src0_rows")
        src_rows = sem("src_rows")
        dst_rows = sem("dst_rows")
        rows_turned = sem("rows_turned")
        srcI0_ok = sem("srcI0_ok")
        srcI_ok = sem("srcI_ok")
        rel_ok = sem("rel_ok")
        hT_made = sem("hT_made")
        hT_ok = sem("hT_ok")
        er_rounds = sem("er_rounds")
        er_ok = sem("er_ok")
        erg_spread = sem("erg_spread")
        raw_var = sem("raw_var")
        raw_root = sem("raw_root")
        odd_ok = sem("odd_ok")
        odd_sum = sem("odd_sum")
        flag_ok = sem("flag_ok")
        lent_free = sem("lent_free")
        acc_zeroed = sem("acc_zeroed")
        v_steps = sem("v_steps")
        e_ok = sem("e_ok")
        onehot_ok = sem("onehot_ok")
        tiles_turned = sem("tiles_turned")
        tiles_ok = sem("tiles_ok")
        scores_made = sem("scores_made")
        scores_ok = sem("scores_ok")
        drow_free = sem("drow_free")
        leaky_ok = sem("leaky_ok")
        scores_turned = sem("scores_turned")
        scans_ok = sem("scans_ok")
        ends_turned = sem("ends_turned")
        carry_ok = sem("carry_ok")
        carry_turned = sem("carry_turned")
        open_diff = sem("open_diff")
        open_exp = sem("open_exp")
        open_all = sem("open_all")
        max_ok = sem("max_ok")
        max_turned = sem("max_turned")
        diff_ok = sem("diff_ok")
        p_ok = sem("p_ok")
        scaled_ok = sem("scaled_ok")
        sums_made = sem("sums_made")
        sums_added = sem("sums_added")
        z_made = sem("z_made")
        z_ok = sem("z_ok")
        zT_made = sem("zT_made")
        zT_ok = sem("zT_ok")
        bn_step = sem("bn_step")
        bn_sum = sem("bn_sum")
        bn_root = sem("bn_root")
        root_warm = sem("root_warm")
        bn_ok = sem("bn_ok")
        z_normed = sem("z_normed")
        z_back = sem("z_back")
        y_ok = sem("y_ok")
        q_init = sem("q_init")
        q_cleared = sem("q_cleared")
        q_src = sem("q_src")
        q_dst = sem("q_dst")
        q_row = sem("q_row")
        q_ea = sem("q_ea")
        q_h = sem("q_h")
        q_er = sem("q_er")
        q_old = sem("q_old")
        q_diag = sem("q_diag")
        q_scores = sem("q_scores")
        q_diff = sem("q_diff")
        q_exp = sem("q_exp")
        q_terms = sem("q_terms")
        q_sum = sem("q_sum")
        q_new = sem("q_new")
        q_stored = sem("q_stored")
        q_free = sem("q_free")
        q_state_in = sem("q_state_in")
        q_state_turned = sem("q_state_turned")
        q_state_ok = sem("q_state_ok")
        q_done = sem("q_done")
        r_steps = sem("r_steps")
        r_made = sem("r_made")
        r_ok = sem("r_ok")
        r_turned = sem("r_turned")
        r_kept = sem("r_kept")

        tln_rep = view(accf, [[1, RG * H * P]], NB * F)

        def base_regs(c, g0, g1):
            return list(nc.values_load_multi_w_load_instructions(
                bases[0:1, c * CG + g0:c * CG + g1], engines=[mybir.EngineType.DVE], min_val=0, max_val=N,
                skip_runtime_bounds_check_because="bases was clamped to [0, N] when it was made")[1])

        def groups_in(c):
            return min(CG, NGR - c * CG)

        def sums_of(c):
            return [(0, 8), (8, groups_in(c))]

        def groups_of(c, k):
            return range(k * GQ, min((k + 1) * GQ, groups_in(c)))

        def gathers_upto(c, k):
            return sum(EPP * len(groups_of(i, k)) for i in range(c % 2, c + 1, 2))

        def bond_dmas(c):
            return 2 if (c + 1) * CHUNK > E else 1

        def bonds_upto(c):
            return sum(bond_dmas(i) for i in range(c % 3, c + 1, 3))

        RB = 512 // (RP * EPP)
        BATCH = [(g, min(RG, g + RB)) for g in range(0, RG, RB)]
        NRT = len(BATCH)

        def columns(t, g0, g1):
            return view(t[:, g0 * RP, :], [[RP * EPP, g1 - g0], [1, EPP], [EPP, RP]])

        def bank_rows(n, sets):
            return pt[n % 2][:, 0:sets * EPP * RP].rearrange("p (g j k) -> p g j k", j=EPP, k=RP)

        def if_flag(eng, which):
            eng.wait_ge(flag_ok, 1)
            r = nc.values_load(flag, engines=[which], min_val=0, max_val=1)
            return eng.If(r != 0)

        def z_bank(b):
            return {NZ - 4: po[0], NZ - 3: po[1], NZ - 1: po[0]}.get(b, p_q)

        assert z_upto(NCH - 2) == NZ - 4

        def z_turned(b):
            return z_bank(b)[:, NR * H * F1:NR * H * F1 + NP_]

        def z_seen(c):
            return list(range(z_upto(c - 2), z_upto(c - 1)))

        HT = [(i, min(i + 4, NB // EPP)) for i in range(0, NB // EPP, 4)]

        HT_OF = [[n for n, (i, _) in enumerate(HT) if b0 <= i * EPP < b1] for b0, b1 in QS]
        assert all(EPP * HT[n][1] <= b1 for ns, (_, b1) in zip(HT_OF, QS) for n in ns)

        def hT(n):
            return view(eT[:, :, :], [[NP_, 4], [1, NP_]], (n % NQ) * 4 * P)

        def ht_bank(n):
            return view(pt[n % 2][:, :], [[NP_, 4], [1, NP_]])

        ENG = mybir.EngineType

        block = ctx.enter_context(nc.Block())

        @block.sync
        def _(sp):
            fullg = FULL // RP
            rest = FULL - fullg * RP
            sp.dma_start(srow_i[0:RP, 0:RB, :],
                         src[0:RB * RP * GROUP].rearrange("(g p e) -> p g e", p=RP, e=GROUP)).then_inc(src0_in, 16)
            sp.wait_ge(pad_zeroed, 1)
            sp.dma_start(srow_i[0:RP, RB:fullg, :],
                         src[RB * RP * GROUP:fullg * RP * GROUP].rearrange("(g p e) -> p g e", p=RP, e=GROUP)
                         ).then_inc(src_in, 16)
            sp.dma_start(srow_i[0:rest, fullg, :],
                         src[fullg * RP * GROUP:FULL * GROUP].rearrange("(p e) -> p e", e=GROUP)).then_inc(src_in, 16)
            sp.dma_start(srow_i[rest:rest + 1, fullg, 0:TAIL],
                         src[FULL * GROUP:E].rearrange("(p e) -> p e", p=1)).then_inc(src_in, 16)
            sp.dma_start(dst_pad[1:1 + E].rearrange("(a b) -> a b", a=16),
                         dst[0:E].rearrange("(a b) -> a b", a=16)).then_inc(dpad_in, 16)
            sp.wait_ge(ident_ok, 1)
            sp.dma_start(dst_pad[1 + E:EPAD + 2].rearrange("(p e) -> p e", p=1), padc[:, :]).then_inc(dpad_in, 16)
            sp.dma_start(dst_pad[0:1].rearrange("(p e) -> p e", p=1), neg1[:, :]).then_inc(dpad_in, 16)
            sp.wait_ge(dpad_in, 48)
            sp.dma_start(drw_i[0:RP], bass.AP(dst_pad.tensor, 1, [[GROUP, RP], [RP * GROUP, RG], [1, GW]])).then_inc(drw_in, 16)
            with nc.allow_non_contiguous_dma(reason="first dst of each group"):
                sp.dma_start(bases[:, :], bass.AP(dst_pad.tensor, 1, [[1, 1], [GROUP, NGP], [1, 1]])).then_inc(bases_in, 16)

            def load_chunk(c):
                q = c % 3
                if c >= 3:
                    sp.wait_ge(sums_made, 2 * (c - 2))
                ng = min(CG, FULL - c * CG)
                sp.dma_start(edge[q].rearrange("p (g j) f -> p g (j f)", j=EPP)[:, 0:ng, :],
                             ea[c * CHUNK:c * CHUNK + ng * GROUP, :].rearrange("(g p j) f -> p g (j f)", p=P, j=EPP)
                             ).then_inc(ea_in[q], 16)
                if bond_dmas(c) == 2:
                    sp.dma_start(edge[q].rearrange("p (g j) f -> p g (j f)", j=EPP)[0:TAIL // EPP, ng, :],
                                 ea[FULL * GROUP:E, :].rearrange("(p j) f -> p (j f)", j=EPP)).then_inc(ea_in[q], 16)
                if c >= 1:
                    sp.wait_ge(drow_free, c)
                for hd in range(H):
                    sp.dma_start(drow2_i[hd * CG:(hd + 1) * CG, :],
                                 bass.AP(dst_pad.tensor, c * CHUNK, [[GROUP, CG], [1, GROUP + 2]])).then_inc(drow_in, 16)

            load_chunk(0)
            for i, (b0, b1) in enumerate(QS):
                sp.wait_ge(h_ok, i + 1)
                for p0, p1 in zip(PS, PS[1:]):
                    sp.dma_start(h_tab.rearrange("(p b) f -> p b f", b=NB)[p0:p1, b0:b1], xln[p0:p1, b0:b1]
                                 ).then_inc(htab_in, 16)
            sp.wait_ge(er_ok, 1)
            for p0, p1 in zip(PS, PS[1:]):
                sp.dma_start(er_tab[0:N * H].rearrange("(p b) -> p b", b=NB * H)[p0:p1],
                             er[p0:p1].rearrange("p b h -> p (b h)")).then_inc(ertab_in, 16)
            sp.dma_start(er_tab[N * H:(EW_ROWS + WIN) * H].rearrange("(p e) -> p e", p=1), zrow[:, :]).then_inc(ertab_in, 16)
            sp.wait_ge(ertab_in, 48)
            sp.dma_start(er_win[:, :], bass.AP(er_tab.tensor, 0, [[H, EW_ROWS], [1, WIN * H]])).then_inc(erwin_in, 16)
            for c in range(1, NCH):
                load_chunk(c)
            sp.wait_ge(sums_made, 2 * (NCH - 1))
            for p0, p1 in zip(PS, PS[1:]):
                sp.dma_start(xres[p0:p1], x.rearrange("(b p r) f -> p b (r f)", p=NP_, r=NR)[p0:p1]).then_inc(xres_in, 16)
            sp.wait_ge(sums_added, 2 * NCH)
            with if_flag(sp, ENG.SP):
                sp.wait_ge(q_init, 1)
                sp.dma_start(state_tab.rearrange("(p b) c -> p b c", p=GT), view(g_init, [[0, N // GT], [1, SROW]])
                             ).then_inc(q_cleared, 16)
                with sp.Fori(0, E // GT) as i:
                    sp.wait_ge(q_free, i + 1)
                    for t, sm, a in ((g_src, q_src, src), (g_dst, q_dst, dst)):
                        sp.dma_start(t, a[bass.ds(i * GT, GT)].rearrange("(p o) -> p o", o=1)).then_inc(sm, 16)
                    row = dst[bass.ds(i * GT, GT)]
                    sp.dma_start(g_row_i, row.rearrange("(o e) -> o e", o=1).broadcast_to([GT, GT])).then_inc(q_row, 16)
                    sp.dma_start(g_ea, ea[bass.ds(i * GT, GT), :]).then_inc(q_ea, 16)
                sp.wait_ge(q_free, E // GT + 1)
                with sp.Fori(0, N // GT) as b:
                    sp.wait_ge(q_state_turned, b + 1)
                    sp.dma_start(g_old, state_tab[bass.ds(b * GT, GT), :]).then_inc(q_state_in, 16)
            for i, (b0, b1) in enumerate(OUT):
                sp.wait_ge(y_ok, 1 + [t1 for _, t1 in TURN].index(b1))
                for p0, p1 in zip(PS, PS[1:]):
                    sp.dma_start(out.rearrange("(b p r) f -> p b (r f)", p=NP_, r=NR)[p0:p1, b0:b1],
                                 xres[p0:p1, b0:b1]).then_inc(out_in, 16)
            sp.wait_ge(htab_in, 32 * len(QS))
            sp.wait_ge(erwin_in, 16)
            sp.wait_ge(out_in, 32 * len(OUT))

        @block.gpsimd
        def _(pool):
            nc.gpsimd.memset(padc[:, :], N).then_inc(const_ok, 1)
            nc.gpsimd.memset(neg1[:, :], -1).then_inc(const_ok, 1)
            nc.gpsimd.memset(ident[:, :], 0.0).then_inc(const_ok, 1)
            nc.gpsimd.iota(iota_i[:, :], [[1, WIN]], base=0, channel_multiplier=0).then_inc(const_ok, 1)
            pool.wait_ge(const_ok, 4)
            nc.gpsimd.affine_select(out=ident[:, :], in_=ident[:, :], compare_op=ALU.not_equal, fill=1.0, base=0,
                                    pattern=[[-1, P]], channel_multiplier=1).then_inc(ident_ok, 1)
            nc.gpsimd.iota(due_all[:, 0:NCH - LAG - 1], [[ZBL, NCH - LAG - 1]], base=ZBL, channel_multiplier=0
                           ).then_inc(const_ok, 1)
            c = NCH - 1
            nc.gpsimd.iota(due_all[:, c - LAG:c - LAG + 1], [[0, 1]], base=ZBL * z_upto(c), channel_multiplier=0
                           ).then_inc(const_ok, 1)
            def gather(c, k):
                q = c % 2
                if c >= 2:
                    pool.wait_ge(e_ok, NQ * (c - 2) + k + 1)
                for g in groups_of(c, k):
                    for j in range(EPP):
                        pool.indirect_dma_start(out=gat[q][:, g * EPP + j, :], out_offset=None,
                                                in_=x if c < RAW else h_tab,
                                                in_offset=bass.IndirectOffsetOnAxis(ap=srcI[:, c * CG + g, j:j + 1], axis=0)
                                                ).then_inc(gat_in[q][k], 16)

            pool.wait_ge(srcI0_ok, 1)
            for c in range(RAW):
                for k in range(NQ):
                    gather(c, k)
            pool.wait_ge(srcI_ok, NRT - 1)
            pool.wait_ge(htab_in, 32 * len(QS))
            gather(RAW, 0)
            gather(RAW, 1)
            pool.wait_ge(erwin_in, 16)
            pool.wait_ge(drw_in, 16)
            for g in range(RG):
                pool.indirect_dma_start(out=erg[0:RP, g, :], out_offset=None, in_=er_win,
                                        in_offset=bass.IndirectOffsetOnAxis(ap=drw_i[0:RP, g, 0:1], axis=0)
                                        ).then_inc(erg_in, 16)
            for c in range(RAW, NCH):
                for k in range(2 * (c == RAW), NQ):
                    gather(c, k)
            pool.wait_ge(sums_added, 2 * NCH)
            with if_flag(pool, ENG.Pool):
                def wait_for(producer, count):
                    pool.wait_ge(producer, count)
                    pool.sem_clear(producer)

                at = bass.IndirectOffsetOnAxis
                pool.wait_ge(q_init, 1)
                nc.gpsimd.affine_select(out=g_below, in_=ones[0:GT, 0:GT], compare_op=ALU.is_gt, fill=0.0, base=0,
                                        pattern=[[-1, GT]], channel_multiplier=1).then_inc(q_free, 1)
                pool.wait_ge(q_cleared, 16)
                with pool.Fori(0, E // GT) as i:
                    wait_for(q_src, 16)
                    pool.indirect_dma_start(out=g_h, out_offset=None, in_=h_tab,
                                            in_offset=at(ap=g_src, axis=0)).then_inc(q_h, 16)
                    wait_for(q_dst, 16)
                    pool.indirect_dma_start(out=g_er, out_offset=None, in_=er_tab.rearrange("(n h) -> n h", h=H),
                                            in_offset=at(ap=g_dst, axis=0)).then_inc(q_er, 16)
                    pool.indirect_dma_start(out=g_old, out_offset=None, in_=state_tab,
                                            in_offset=at(ap=g_dst, axis=0)).then_inc(q_old, 16)
                    wait_for(q_new, 1)
                    pool.indirect_dma_start(out=state_tab, out_offset=at(ap=g_to, axis=0), in_=g_new, in_offset=None,
                                            bounds_check=N - 1, oob_is_err=False).then_inc(q_stored, 16)
                    pool.wait_ge(q_stored, i * 16 + 16)
                    pool.sem_inc(q_free, 1)

        @block.scalar
        def _(act):
            for i, (b0, b1) in enumerate(QS):
                for p0, p1 in zip(PS, PS[1:]):
                    act.dma_start(xln[p0:p1, b0:b1], x.rearrange("(p b) f -> p b f", b=NB)[p0:p1, b0:b1]
                                  ).then_inc(x_in[i], 16)
            for a in range(2):
                act.dma_start(Wd[a * F:(a + 1) * F, :], W[:, :]).then_inc(w_in, 16)
            for t, v in ((alb[:, :], attn_l), (arb[:, :], attn_r)):
                act.dma_start(t, bass.AP(v.tensor, 0, [[0, P], [1, H * F]])).then_inc(w_in, 16)
            with nc.allow_non_contiguous_dma(reason="one feature per partition"):
                for i, v in enumerate((gamma, beta)):
                    for r in range(NR):
                        act.dma_start(gb[r * F:(r + 1) * F, i:i + 1], v.rearrange("(f o) -> f o", o=1)).then_inc(w_in, 16)
            def square(i):
                b0, b1 = QS[i]
                act.wait_ge(ln_centred, i + 1)
                nc.scalar.activation(xln[0:NP_, b0:b1], tln[0:NP_, b0:b1], ACT.Square).then_inc(ln_squared, 1)

            def root(i):
                b0, b1 = QS[i]
                act.wait_ge(ln_var, i + 1)
                nc.scalar.activation(ln_b[0:NP_, b0:b1], ln_a[0:NP_, b0:b1], ACT.Sqrt).then_inc(ln_root, 1)

            def evacuate(n):
                act.wait_ge(hT_made, n + 1)
                if n >= NQ:
                    act.wait_ge(er_rounds, n - NQ + 1)
                w = HT[n][1] - HT[n][0]
                nc.scalar.activation(hT(n)[:, 0:w, :], ht_bank(n)[:, 0:w, :], ACT.Copy).then_inc(hT_ok, 1)

            def root_of_gathered(c):
                act.wait_ge(raw_var, c + 1)
                nc.scalar.activation(g_var, g_var, ACT.Sqrt).then_inc(raw_root, 1)

            square(0)
            square(1)
            root(0)
            square(2)
            root(1)
            square(3)
            for n in HT_OF[0]:
                evacuate(n)
            root(2)
            root(3)
            for n in HT_OF[1] + HT_OF[2] + HT_OF[3][:1]:
                evacuate(n)
            root_of_gathered(0)
            for n in HT_OF[3][1:]:
                evacuate(n)
            act.wait_ge(src_in, 48)
            nc.scalar.activation(srow[0:RP, RB:RG], srow_i[0:RP, RB:RG], ACT.Copy).then_inc(src_rows, 1)
            for n, (g0, g1) in list(enumerate(BATCH))[1:]:
                act.wait_ge(rows_turned, n + 1)
                nc.scalar.activation(columns(srcI, g0, g1), bank_rows(n, g1 - g0), ACT.Copy).then_inc(srcI_ok, 1)
            act.wait_ge(htab_in, 32 * len(QS))
            act.wait_ge(er_rounds, len(HT))
            for a, b in CLEAR[0:2]:
                nc.scalar.activation(accf[0:F1, a:b], view(zero1[0:F1, :], [[0, b - a]]), ACT.Copy).then_inc(acc_zeroed, 1)
            root_of_gathered(1)
            for a, b in CLEAR[2:4]:
                if (a, b) == CLEAR[3]:
                    act.wait_ge(lent_free, 1)
                nc.scalar.activation(accf[0:F1, a:b], view(zero1[0:F1, :], [[0, b - a]]), ACT.Copy).then_inc(acc_zeroed, 1)

            n_tr = [0]

            def front(c, k):
                if c:
                    act.wait_ge(scores_made, NQ * (c - 1) + k + 1)
                for dest, n in ((eT[:, GQ * k:GQ * (k + 1), :], GQ), (ohT[:, GQ // 2 * k:GQ // 2 * (k + 1), :], GQ // 2)):
                    n_tr[0] += 1
                    act.wait_ge(tiles_turned, n_tr[0])
                    nc.scalar.activation(dest, pt[(n_tr[0] - 1) % 2][:, 0:n * P].rearrange("p (a b) -> p a b", b=P),
                                         ACT.Copy).then_inc(tiles_ok, 1)

            def z_keep(b, turned, kept):
                act.wait_ge(turned, b + 1)
                nc.scalar.activation(zT[:, b, :], z_turned(b), ACT.Copy).then_inc(kept, 1)

            for k in range(NQ - 1):
                front(0, k)
            for c in range(NCH):
                if c == NCH - 1:
                    z_keep(NZ - 5, zT_made, zT_ok)
                    z_keep(NZ - 4, zT_made, zT_ok)
                front(c, NQ - 1)
                act.wait_ge(scores_made, NQ * (c + 1))
                if c:
                    act.wait_ge(leaky_ok, c)
                nc.scalar.activation(s_raw[:, :, :, :].rearrange("p h g j -> p g j h"),
                                     S_ps.rearrange("p (g j h) -> p g j h", j=EPP, h=H), ACT.Copy).then_inc(scores_ok, 1)
                for b in z_seen(c) if c < NCH - 1 else [NZ - 3]:
                    z_keep(b, zT_made, zT_ok)
                if c + 1 < NCH:
                    front(c + 1, 0)
                act.wait_ge(open_diff, c + 1)
                if c:
                    act.wait_ge(open_all, c)
                nc.scalar.activation(fexp[:, :], fdif[:, :], ACT.Exp).then_inc(open_exp, 1)
                act.wait_ge(diff_ok, c + 1)
                if c:
                    act.wait_ge(scaled_ok, c)
                nc.scalar.activation(p_e[:, :, :], sdif[:, :, :, :].rearrange("p h g j -> p h (g j)"), ACT.Exp
                                     ).then_inc(p_ok, 1)
                if c + 1 < NCH:
                    for k in range(1, NQ - 1):
                        front(c + 1, k)
            z_keep(NZ - 2, zT_made, zT_ok)
            z_keep(NZ - 1, zT_made, zT_ok)
            with if_flag(act, ENG.Activation):
                with act.Fori(0, E // GT) as i:
                    act.wait_ge(q_diff, i + 1)
                    nc.scalar.activation(g_ex, g_dif, ACT.Exp).then_inc(q_exp, 1)
                for b in range(NZ):
                    z_keep(b, r_turned, r_kept)
            nc.scalar.activation(fexp[:, 0:1], ones[0:1, 0:1], ACT.Sqrt).then_inc(root_warm, 1)
            act.wait_ge(bn_step, 3)
            nc.scalar.activation(col[:, STD], col[:, VAR], ACT.Sqrt).then_inc(bn_root, 1)
            act.wait_ge(bn_ok, 1)
            for b0, b1 in AFF:
                nc.scalar.activation(zT[:, b0:b1, :], zT[:, b0:b1, :], ACT.Identity, bias=col[:, SHIFT],
                                     scale=col[:, SCALE]).then_inc(z_normed, 1)

        @block.tensor
        def _(pe):
            mm = nc.tensor.matmul
            def z_block(b, made, kept):
                before = [a for a in range(b) if z_bank(a) is z_bank(b)]
                if before:
                    pe.wait_ge(kept, before[-1] + 1)
                for r in range(NR):
                    for hd in range(H):
                        c0 = (r * H + hd) * F1
                        m = mm(z_bank(b)[0:NP_, c0:c0 + F1], view(acc[0:F1, hd, 0:1], [[NR, NP_]], b * ZBL + r),
                               wz[:, hd, :], start=True, stop=True)
                m.then_inc(made, 1)

            def z_turn(b, read, turned):
                pe.wait_ge(read, b + 1)
                nc.tensor.transpose(z_turned(b), zn[0:NP_, b % 2].rearrange("p r f -> p (r f)"), ident[0:NP_, 0:NP_]
                                    ).then_inc(turned, 1)

            def copied_out(n):
                if n <= NRT:
                    pe.wait_ge(srcI_ok if n > 1 else srcI0_ok, max(n - 1, 1))
                else:
                    pe.wait_ge(rel_ok, n - NRT)

            def er_table():
                copied_out(1)
                pe.wait_ge(wr_ok, 1)
                for n, (i0, i1) in enumerate(HT):
                    pe.wait_ge(h_ok, 1 + [n in ns for ns in HT_OF].index(True))
                    if n >= 2:
                        pe.wait_ge(hT_ok, n - 1)
                    for i in range(i0, i1):
                        m = nc.tensor.transpose(ht_bank(n)[:, i - i0, :],
                                                xln[0:NP_, EPP * i:EPP * (i + 1), :].rearrange("p b f -> p (b f)"),
                                                ident[0:NP_, 0:NP_])
                    m.then_inc(hT_made, 1)
                    if n:
                        er_of(n - 1)
                er_of(len(HT) - 1)

            def er_of(n):
                pe.wait_ge(hT_ok, n + 1)
                for i in range(*HT[n]):
                    m = mm(p_s[0:NP_, i * EPP * H:(i + 1) * EPP * H], hT(n)[:, i - HT[n][0], :], wr2[:, :],
                           start=True, stop=True)
                m.then_inc(er_rounds, 1)

            pe.wait_ge(ident_ok, 1)
            n_rt = 0
            for arr in (srow, drw):
                for i, (g0, g1) in enumerate(BATCH):
                    pe.wait_ge((dst_rows if arr is drw else src_rows if i else src0_rows), 1)
                    if n_rt >= 2:
                        copied_out(n_rt - 1)
                    for g in range(g0, g1):
                        for j in range(EPP):
                            m = mm(bank_rows(n_rt, g1 - g0)[:, g - g0, j, :],
                                   view(arr[0:RP], [[EPP, P]], g * (GW if arr is drw else GROUP) + j),
                                   ident[0:RP, 0:RP], start=True, stop=True)
                    m.then_inc(rows_turned, 1)
                    n_rt += 1
                    if n_rt == 1:
                        er_table()
                if arr is srow:
                    pe.wait_ge(wr_ok, 1)
                    for i in range(H):
                        m = mm(p_q[:, i * F:(i + 1) * F], wB[:, i, :], ident[0:F, 0:F], start=True, stop=True)
                    m.then_inc(wl_turned, 1)
            pe.wait_ge(odd_ok, 1)
            mm(p_s[:, 0:1], ones[0:RP, :], odd_n[0:RP, 0:1], start=True, stop=True).then_inc(odd_sum, 1)
            pe.wait_ge(erg_spread, 1)
            for g in range(RG):
                copied_out(n_rt - 1)
                for hd in range(H):
                    m = mm(pt[n_rt % 2][:, hd * RP:(hd + 1) * RP], tln_rep[0:RP, (g * H + hd) * P:(g * H + hd + 1) * P],
                           ident[0:RP, 0:RP], start=True, stop=True)
                m.then_inc(rows_turned, 1)
                n_rt += 1
            copied_out(n_rt)

            n_tr = [0]

            def turn(c, k):
                pe.wait_ge(e_ok, NQ * c + k + 1)
                if k == 0:
                    pe.wait_ge(onehot_ok, c + 1)
                oh = onehot[:, c % 2]
                rows = ([edge[c % 3][:, t:t + EPP, :] for t in range(TQ * k, TQ * (k + 1), EPP)],
                        [oh[:, t:t + 4, :] for t in range(TQ * k, TQ * (k + 1), 4)])
                for tiles in rows:
                    if n_tr[0] >= 2:
                        pe.wait_ge(tiles_ok, n_tr[0] - 1)
                    for i, a in enumerate(tiles):
                        m = nc.tensor.transpose(pt[n_tr[0] % 2][:, i * P:(i + 1) * P], a.rearrange("p t f -> p (t f)"),
                                                ident[:, :])
                    m.then_inc(tiles_turned, 1)
                    n_tr[0] += 1

            def scores(c, k):
                pe.wait_ge(tiles_ok, n_tr[0])
                if k == 0 and c:
                    pe.wait_ge(scores_ok, c)
                for g in range(GQ * k, GQ * (k + 1)):
                    n = c * CG + g
                    if g % 2 == 0:
                        mm(S_ps[:, g * 4:g * 4 + 8], ohT[:, g // 2, :],
                           er_bd[:, n:n + 2, :, :].rearrange("p k j h -> p (k j h)"),
                           start=True, stop=False, skip_group_check=True)
                    m = mm(S_ps[:, g * 4:g * 4 + 4], eT[:, g, :], wl2[:, :], start=False, stop=True,
                           skip_group_check=True)
                m.then_inc(scores_made, 1)

            for k in range(NQ - 1):
                turn(0, k)
                scores(0, k)
            for c in range(NCH):
                new_z = range(z_upto(c - 1), z_upto(c)) if c >= LAG else range(0)
                if c == NCH - 1:
                    pe.wait_ge(sums_added, 2 * c)
                    z_block(NZ - 4, z_made, zT_ok)
                    z_block(NZ - 3, z_made, zT_ok)
                    z_turn(NZ - 5, z_ok, zT_made)
                    z_block(NZ - 2, z_made, zT_ok)
                    z_turn(NZ - 4, z_ok, zT_made)
                turn(c, NQ - 1)
                scores(c, NQ - 1)
                for b in z_seen(c) if c < NCH - 1 else [NZ - 3]:
                    z_turn(b, z_ok, zT_made)
                pe.wait_ge(leaky_ok, c + 1)
                for j in range(EPP):
                    m = mm(view(sT_ps, [[EPP, P]], j), s_lr[:, :, :, j].rearrange("p h g -> p (h g)"), ident[:, :],
                           start=True, stop=True)
                m.then_inc(scores_turned, 1)
                if c < NCH - 1:
                    for b in new_z:
                        pe.wait_ge(sums_added, 2 * c)
                        z_block(b, z_made, zT_ok)
                pe.wait_ge(scans_ok, c + 1)
                for i, col in enumerate(row_ends):
                    m = mm(row_ps[:, i * R2:(i + 1) * R2], col, ident[0:R2, 0:R2], start=True, stop=True)
                m.then_inc(ends_turned, 1)
                if c + 1 < NCH:
                    turn(c + 1, 0)
                pe.wait_ge(carry_ok, c + 1)
                for i, t in enumerate((cin, cout)):
                    m = mm(cc_ps[:, i:i + 1], t[:, :, :].rearrange("p h g -> p (h g)"), ones[0:1, 0:1],
                           start=True, stop=True)
                m.then_inc(carry_turned, 1)
                pe.wait_ge(open_exp, c + 1)
                mm(fb_ps, ones[0:1, 0:F1], fexp[:, :], start=True, stop=True).then_inc(open_all, 1)
                pe.wait_ge(max_ok, c + 1)
                for j in range(EPP):
                    m = mm(M_ps.rearrange("p (r j) -> p r j", j=EPP)[:, :, j], view(mx[:, :], [[EPP, P]], j),
                           ident[0:R2, 0:R2], start=True, stop=True)
                m.then_inc(max_turned, 1)
                if c + 1 < NCH:
                    scores(c + 1, 0)
                pe.wait_ge(scaled_ok, c + 1)
                if c == NCH - 1:
                    pe.wait_ge(zT_ok, NZ - 2)
                for g0, g1 in sums_of(c):
                    if c and g0 % 8 == 0:
                        pe.wait_ge(sums_added, 2 * (c - 1) + g0 // 8 + 1)
                    bank = po[g0 // 8]
                    for g in range(g0, g1):
                        for j in range(EPP):
                            t = g * EPP + j
                            mm(bank[0:F, (g % 8) * H * WIN:(g % 8 + 1) * H * WIN], edge[c % 3][:, t, :],
                               scaled[:, t, :, :].rearrange("p h w -> p (h w)"), start=(j == 0), stop=(j == EPP - 1))
                    for j in range(EPP):
                        m = mm(bank[F:F1, (g0 % 8) * H * WIN:(g0 % 8 + g1 - g0) * H * WIN], ones[:, 0:1],
                               view(scaled[:, g0 * EPP + j, 0, :], [[EPP * H * WIN, g1 - g0], [1, H * WIN]]),
                               start=(j == 0), stop=(j == EPP - 1))
                    m.then_inc(sums_made, 1)
                if c + 1 < NCH:
                    for k in range(1, NQ - 1):
                        turn(c + 1, k)
                        scores(c + 1, k)
            z_turn(NZ - 2, z_ok, zT_made)
            pe.wait_ge(sums_added, 2 * NCH)
            z_block(NZ - 1, z_made, zT_ok)
            z_turn(NZ - 1, z_ok, zT_made)
            with if_flag(pe, ENG.PE):
                with pe.Fori(0, E // GT) as i:
                    pe.wait_ge(q_diag, i + 1)
                    mm(p_s[0:GT, 0:H * GT], ones[0:GT, 0:GT], g_diag.rearrange("p h e -> p (h e)"),
                       start=True, stop=True).then_inc(q_scores, 1)
                    pe.wait_ge(q_terms, i + 1)
                    mm(p_m[0:GT, 0:H * F1], g_same, g_u.rearrange("p h f -> p (h f)"),
                       start=True, stop=True).then_inc(q_sum, 1)
                pe.sem_inc(q_state_turned, 1)
                with pe.Fori(0, N // GT) as b:
                    pe.wait_ge(q_state_in, b * 16 + 16)
                    pe.wait_ge(q_state_ok, b + 1)
                    for hd in range(H):
                        m = mm(p_r[0:F1, hd * GT:(hd + 1) * GT], g_old[:, H + hd * F1:H + (hd + 1) * F1],
                               ident[0:GT, 0:GT], start=True, stop=True)
                    m.then_inc(q_state_turned, 1)
                pe.wait_ge(q_done, 1)
                for b in range(NZ):
                    z_block(b, r_made, r_kept)
                    z_turn(b, r_ok, r_turned)
            every, mean, dev = p_s[:, 0:F], p_s[:, F:F + 1], p_s[:, F + 1:F + 2]
            pairs = zz[0:NP_].rearrange("p r f -> p (r f)")
            pe.wait_ge(bn_step, 1)
            mm(every, ones[0:NP_, :], zz[0:NP_, 0, :], start=True, stop=True)
            mm(mean, pairs, ones[0:NP_, 0:1], start=True, stop=True).then_inc(bn_sum, 1)
            pe.wait_ge(bn_step, 2)
            mm(dev, pairs, ones[0:NP_, 0:1], start=True, stop=True).then_inc(bn_sum, 1)
            for n, (b0, b1) in enumerate(TURN):
                pe.wait_ge(z_normed, 1 + [b0 < a1 for _, a1 in AFF].index(True))
                if n >= len(out_banks):
                    pe.wait_ge(y_ok, n - len(out_banks) + 1)
                for b in range(b0, b1):
                    m = nc.tensor.transpose(out_banks[n % len(out_banks)][0:NP_, (b - b0) * NR * F:(b - b0 + 1) * NR * F],
                                            zT[:, b, :], ident[:, :])
                m.then_inc(z_back, 1)

        @block.vector
        def _(dve):
            v = nc.vector
            done = [v_steps, 0]

            def step(ins):
                done[1] += 1
                ins.then_inc(done[0], 1)
                dve.wait_ge(done[0], done[1])

            def also(ins):
                done[1] += 1
                ins.then_inc(done[0], 1)

            def signal(s):
                dve.sem_inc(s, 1)

            step(v.memset(srow_i[0:RP, RG - 1, :], 0))
            signal(pad_zeroed)
            step(v.memset(ones[:, :], 1.0))
            dve.wait_ge(src0_in, 16)
            step(v.tensor_copy(srow[0:RP, 0:RB], srow_i[0:RP, 0:RB]))
            signal(src0_rows)
            step(v.memset(zero1[:, :], 0.0))
            step(v.memset(zrow[:, :], 0.0))
            step(v.memset(wl2[:, :], 0.0))
            step(v.memset(wr2[:, :], 0.0))
            step(v.memset(quarter, 0.0))
            for r in range(4):
                step(v.memset(view(quarter[r * WIN:(r + 1) * WIN], [[2 * EPP, RP // 2]], (r // EPP) * EPP + r % EPP), 1.0))
            step(v.memset(wz[:, :, :], 0.0))
            step(v.memset(tail_in[:, :, 0:1], -BIG))
            step(v.memset(head_in[:, :, CG:CG + 1], -BIG))
            dve.wait_ge(rows_turned, 1)
            step(v.tensor_copy(columns(srcI, *BATCH[0]), bank_rows(0, BATCH[0][1])))
            signal(srcI0_ok)

            def make_e(c, k):
                q, t = c % 2, slice(TQ * k, TQ * (k + 1))
                dve.wait_ge(gat_in[q][k], 16 * gathers_upto(c, k))
                if k == 0:
                    dve.wait_ge(ea_in[c % 3], 16 * bonds_upto(c))
                step(v.tensor_tensor(edge[c % 3][:, t], gat[q][:, t], edge[c % 3][:, t], ALU.add))
                signal(e_ok)

            def make_e_raw(c):
                h = gat[c]
                for k in range(NQ):
                    dve.wait_ge(gat_in[c][k], 16 * gathers_upto(c, k))
                per_row = [[1, CT], [0, F]]
                step(v.tensor_reduce(g_mean, h, AX.X, ALU.add))
                step(v.tensor_scalar(g_mean, g_mean, 1.0 / F, None, ALU.mult))
                step(v.tensor_tensor(h, h, view(g_mean, per_row), ALU.subtract))
                step(v.tensor_tensor(g_sq, h, h, ALU.mult))
                step(v.tensor_reduce(g_var, g_sq, AX.X, ALU.add))
                step(v.tensor_scalar(g_var, g_var, 1.0 / F, LN_EPS, ALU.mult, ALU.add))
                signal(raw_var)
                dve.wait_ge(raw_root, c + 1)
                step(v.reciprocal(g_var, g_var))
                step(v.scalar_tensor_tensor(h, h, 0.0, view(g_var, per_row), ALU.max, ALU.mult))
                dve.wait_ge(ea_in[c], 16)
                step(v.tensor_tensor(edge[c], h, edge[c], ALU.add))
                dve.sem_inc(e_ok, NQ)

            def centre(i):
                b0, b1 = QS[i]
                dve.wait_ge(x_in[i], 32)
                step(v.tensor_reduce(ln_a[0:NP_, b0:b1], xln[0:NP_, b0:b1], AX.X, ALU.add))
                step(v.tensor_scalar(ln_m[0:NP_, b0:b1], ln_a[0:NP_, b0:b1], 1.0 / F, None, ALU.mult))
                step(v.tensor_tensor(tln[0:NP_, b0:b1], xln[0:NP_, b0:b1],
                                     view(ln_m[0:NP_, b0:b1], [[1, b1 - b0], [0, F]]), ALU.subtract))
                signal(ln_centred)

            def variance(i):
                b0, b1 = QS[i]
                dve.wait_ge(ln_squared, i + 1)
                step(v.tensor_reduce(ln_a[0:NP_, b0:b1], xln[0:NP_, b0:b1], AX.X, ALU.add))
                step(v.tensor_scalar(ln_a[0:NP_, b0:b1], ln_a[0:NP_, b0:b1], 1.0 / F, LN_EPS, ALU.mult, ALU.add))
                signal(ln_var)

            def normed(i):
                b0, b1 = QS[i]
                dve.wait_ge(ln_root, i + 1)
                step(v.reciprocal(ln_a[0:NP_, b0:b1], ln_b[0:NP_, b0:b1]))
                step(v.scalar_tensor_tensor(xln[0:NP_, b0:b1], tln[0:NP_, b0:b1], 0.0,
                                            view(ln_a[0:NP_, b0:b1], [[1, b1 - b0], [0, F]]), ALU.max, ALU.mult))
                signal(h_ok)

            centre(0)
            centre(1)
            dve.wait_ge(w_in, 16 * (4 + 2 * NR))
            for i, ab in enumerate((alb, arb)):
                step(v.tensor_tensor(wtmp[:, :], Wd[:, :], ab[:, :], ALU.mult))
                step(v.tensor_reduce(wlr[:, i * H:(i + 1) * H], wtmp[:, :].rearrange("p (h d) -> p h d", h=H), AX.X, ALU.add))
            for j in range(EPP):
                step(v.tensor_copy(wl2[j * F:(j + 1) * F, j * H:(j + 1) * H], wlr[j * F:(j + 1) * F, 0:H]))
                step(v.tensor_copy(wr2[j * F:(j + 1) * F, j * H:(j + 1) * H], wlr[j * F:(j + 1) * F, H:2 * H]))
            step(v.tensor_copy(wB[:, :, :], view(wlr[0:F, :], [[1, H], [0, P]])))
            signal(wr_ok)
            variance(0)
            centre(2)
            normed(0)
            variance(1)
            centre(3)
            normed(1)
            variance(2)
            variance(3)
            normed(2)
            normed(3)
            make_e_raw(0)
            for hd in range(H):
                step(v.tensor_copy(wz[0:F, hd, 0:F], Wd[0:F, hd * F:(hd + 1) * F]))
                step(v.memset(wz[F:F1, hd, F:F1], 1.0))
            dve.wait_ge(er_rounds, len(HT))
            step(v.tensor_copy(er[0:NP_].rearrange("p b h -> p (b h)"), p_s[0:NP_, 0:NB * H]))
            signal(er_ok)
            dve.wait_ge(drw_in, 16)
            step(v.tensor_copy(drw[0:RP], drw_i[0:RP]))
            step(v.tensor_copy(ln_a[0:RP, 0:RG], drw[0:RP, :, 0]))
            step(v.tensor_tensor(drw[0:RP], drw[0:RP], view(ln_a[0:RP, 0:RG], [[1, RG], [0, GW]]), ALU.subtract))
            signal(dst_rows)
            dve.wait_ge(wl_turned, 1)
            step(v.tensor_copy(wb[:, :, :], p_q[:, 0:H * F].rearrange("p (i f) -> p i f", f=F)))
            n_rt = NRT
            for g0, g1 in BATCH:
                dve.wait_ge(rows_turned, n_rt + 1)
                step(v.tensor_copy(columns(rel, g0, g1), bank_rows(n_rt, g1 - g0)))
                signal(rel_ok)
                n_rt += 1
            dve.wait_ge(ident_ok, 1)
            step(v.tensor_copy(iota[:, :], iota_i[:, :]))

            def penalties(c):
                dve.wait_ge(drow_in, 32 * (c + 1))
                step(v.tensor_copy(drow[:, :], drow2_i[:, :]))
                signal(drow_free)
                also(v.tensor_tensor(pen[:, :], drow[:, 1:GROUP + 2], drow[:, 0:GROUP + 1], ALU.not_equal))
                own = drow[:, 1:GROUP + 1]
                also(v.tensor_scalar(pen_first[:, :], own, drow[:, 1:2], -BIG, ALU.not_equal, ALU.mult))
                also(v.tensor_scalar(pen_last[:, :], own, drow[:, GROUP:GROUP + 1], -BIG, ALU.not_equal, ALU.mult))
                also(v.tensor_scalar(link[:, 0:1], drow[:, GROUP:GROUP + 1], drow[:, 0:1], -BIG,
                                     ALU.not_equal, ALU.mult))
                step(v.tensor_scalar(link[:, 1:2], drow[:, 1:2], drow[:, GROUP + 1:GROUP + 2], -BIG,
                                     ALU.not_equal, ALU.mult))
                step(v.tensor_scalar(pen[:, :], pen[:, :], -BIG, None, ALU.mult))

            def make_onehot(c):
                q = c % 2
                if c >= 2:
                    dve.wait_ge(scores_made, NQ * (c - 1))
                step(v.tensor_tensor(onehot[:, q, :, :], view(iota[:, :], [[0, CT], [1, WIN]]),
                                     view(rel[:, c * CG, :], [[1, CT], [0, WIN]]), ALU.is_equal))
                signal(onehot_ok)

            make_onehot(0)
            step(v.tensor_tensor(odd, drw[0:RP, :, 1:GW], drw[0:RP, :, 0:GROUP], ALU.is_lt))
            step(v.tensor_reduce(odd_n[0:RP, 0:1], odd, AX.XY, ALU.add))
            step(v.tensor_scalar(odd, drw[0:RP, :, 0:GROUP], float(WIN), None, ALU.is_ge))
            step(v.tensor_reduce(odd_n[0:RP, 1:2], odd, AX.XY, ALU.add))
            step(v.tensor_tensor(odd_n[0:RP, 0:1], odd_n[0:RP, 0:1], odd_n[0:RP, 1:2], ALU.add))
            signal(odd_ok)
            dve.wait_ge(odd_sum, 1)
            step(v.tensor_scalar(flag_n[:, 0:1], p_s[BP:BP + 1, 0:1], 0.0, None, ALU.is_gt))
            dve.wait_ge(bases_in, 16)
            dve.wait_ge(const_ok, 6)
            step(v.tensor_copy(due[:, 0, :], view(bases, [[CG, NCH - LAG]], LAG * CG)))
            step(v.tensor_copy(due[:, 1, :], due_i))
            step(v.tensor_tensor(due[:, 2, :], due[:, 0, :], due[:, 1, :], ALU.is_lt))
            step(v.tensor_reduce(flag_n[:, 1:2], due[:, 2, :], AX.X, ALU.max))
            step(v.tensor_tensor(flag, flag_n[:, 0:1], flag_n[:, 1:2], ALU.max))
            step(v.tensor_scalar(flag_n[:, 0:1], flag, float(N), None, ALU.mult))
            step(v.tensor_scalar(bases, bases, flag_n[:, 0:1], float(N), ALU.max, ALU.min))
            signal(flag_ok)
            penalties(0)
            make_e_raw(1)
            dve.wait_ge(erg_in, 16 * RG)
            for hd in range(H):
                for r in range(4):
                    step(v.tensor_copy(view(tln_rep[0:RP], [[H * P, RG], [1, WIN]], hd * P + r * WIN),
                                       view(erg[0:RP], [[WIN * H, RG], [H, WIN]], hd)))
            signal(erg_spread)
            for g in range(RG):
                dve.wait_ge(rows_turned, n_rt + 1)
                step(v.tensor_tensor(view(er_bd[:, g * RP, 0, :], [[1, H], [EPP * H, RP], [H, EPP]]),
                                     view(pt[n_rt % 2][:, :], [[RP, H], [1, RP], [0, EPP]]),
                                     view(quarter, [[0, H], [EPP, RP], [1, EPP]]), ALU.mult))
                signal(rel_ok)
                n_rt += 1
            dve.wait_ge(htab_in, 32 * len(QS))
            dve.wait_ge(ertab_in, 48)
            signal(lent_free)
            step(v.memset(accf[0:F1, CLEAR[4][0]:CLEAR[4][1]], 0.0))
            step(v.memset(zmean[:, :, :], 0.0))
            step(v.memset(zdev[:, :, :], 0.0))

            def z_block(b, made, read, turned):
                z = z_bank(b)[0:NP_, :]
                n, zb, d = zw[0:NP_], zn[0:NP_, b % 2], zd[0:NP_]
                dve.wait_ge(made, b + 1)
                step(v.tensor_scalar(rden[0:NP_], view(z, [[H * F1, NR], [F1, H]], F), 1e-30, float(H), ALU.max, ALU.mult))
                step(v.reciprocal(rden[0:NP_], rden[0:NP_]))
                step(v.tensor_tensor(n, view(z, [[H * F1, NR], [F1, H], [1, F]]),
                                     view(rden[0:NP_, 0, :], [[H, NR], [1, H], [0, F]]), ALU.mult))
                if b >= 2:
                    dve.wait_ge(turned, b - 1)
                step(v.tensor_tensor(zb, n[:, :, 0, :], n[:, :, 1, :], ALU.add))
                signal(read)
                step(v.tensor_tensor(d, zb, zmean[0:NP_], ALU.subtract))
                step(v.scalar_tensor_tensor(zmean[0:NP_], d, 1.0 / (b + 1), zmean[0:NP_], ALU.mult, ALU.add))
                step(v.tensor_tensor(n[:, :, 0, :], zb, zmean[0:NP_], ALU.subtract))
                step(v.tensor_tensor(d, d, n[:, :, 0, :], ALU.mult))
                step(v.tensor_tensor(zdev[0:NP_], zdev[0:NP_], d, ALU.add))

            def early(c, k):
                if c < AHEAD:
                    if c >= RAW - 1:
                        make_e(c + 1, k)
                elif AHEAD < c < NCH:
                    make_e(c, k)

            for c in range(NCH):
                q = c % 2
                zs = z_seen(c)
                if c == NCH - 1:
                    zs += range(z_upto(c - 1), z_upto(c))
                    while len(zs) > 2:
                        z_block(zs.pop(0), z_made, z_ok, zT_made)
                early(c, NQ - 1)
                if zs:
                    z_block(zs.pop(0), z_made, z_ok, zT_made)
                if c + 1 < NCH:
                    make_onehot(c + 1)
                dve.wait_ge(scores_ok, c + 1)
                step(v.scalar_tensor_tensor(s_lr[:, :, :, :], s_raw[:, :, :, :], NEG_SLOPE, s_raw[:, :, :, :],
                                            ALU.mult, ALU.max))
                signal(leaky_ok)
                base = base_regs(c, 0, 4)
                dve.wait_ge(scores_turned, c + 1)
                also(v.tensor_tensor_scan(fw[:, :], pen[:, 0:GROUP], sT_ps, -BIG, ALU.add, ALU.max))
                step(v.tensor_tensor_scan(view(bw[:, :], [[-1, GROUP]], GROUP - 1),
                                          view(pen[:, :], [[-1, GROUP]], GROUP),
                                          view(sT_ps, [[-1, GROUP]], GROUP - 1), -BIG, ALU.add, ALU.max))
                signal(scans_ok)
                step(v.tensor_tensor(mx[:, :], fw[:, :], bw[:, :], ALU.max))
                early(c + 1, 0)
                dve.wait_ge(ends_turned, c + 1)
                step(v.tensor_copy(fw[0:1, 0:6 * R2], row_ps[:, :]))
                rows = fw[0:1, 0:6 * R2]

                def rw(i, hd):
                    return fw[0:1, i * R2 + hd * CG:i * R2 + (hd + 1) * CG]

                for hd in range(H):
                    also(v.tensor_tensor_scan(tail_in[:, hd, 1:CG + 1], rw(LINKF, hd), rw(TAILC, hd),
                                              tail_in[:, hd, 0:1], ALU.add, ALU.max))
                    (step if hd else also)(v.tensor_tensor_scan(view(head_in[:, hd, :], [[-1, CG]], CG - 1),
                                              view(rw(LINKB, hd), [[-1, CG]], CG - 1),
                                              view(rw(HEADC, hd), [[-1, CG]], CG - 1), -BIG, ALU.add, ALU.max))
                also(v.tensor_tensor(cin[:, :, :], tail_in[:, :, 0:CG],
                                     view(rows, [[CG, H], [1, CG]], CONNF * R2), ALU.add))
                step(v.tensor_tensor(cout[:, :, :], head_in[:, :, 1:CG + 1],
                                     view(rows, [[CG, H], [1, CG]], CONNB * R2), ALU.add))
                signal(carry_ok)
                step(v.tensor_tensor(fmax[:, :, :], cin[:, :, 0:1], head_in[:, :, 0:1], ALU.max))
                step(v.tensor_tensor(fdif[:, :], cin[:, :, 0], fmax[:, :, 0], ALU.subtract))
                signal(open_diff)
                dve.wait_ge(carry_turned, c + 1)
                step(v.tensor_copy(cc[:, :], cc_ps))
                step(v.scalar_tensor_tensor(mx[:, :], pen_first[:, :], cc[:, 0:1], mx[:, :], ALU.add, ALU.max))
                step(v.scalar_tensor_tensor(mx[:, :], pen_last[:, :], cc[:, 1:2], mx[:, :], ALU.add, ALU.max))
                signal(max_ok)
                also(v.tensor_copy(tail_in[:, :, 0:1], tail_in[:, :, CG:CG + 1]))
                base += base_regs(c, 4, 8)
                dve.wait_ge(max_turned, c + 1)
                step(v.tensor_tensor(sdif[:, :, :, :].rearrange("p h g j -> p (h g j)"),
                                     s_lr[:, :, :, :].rearrange("p h g j -> p (h g j)"), M_ps, ALU.subtract))
                signal(diff_ok)
                dve.wait_ge(p_ok, c + 1)
                if c:
                    dve.wait_ge(sums_made, 2 * c)
                step(v.tensor_tensor(scaled[:, :, :, :], view(onehot[:, q, :, :], [[WIN, CT], [0, H], [1, WIN]]),
                                     view(p_e[:, :, :], [[1, CT], [CT, H], [0, WIN]]), ALU.mult))
                signal(scaled_ok)
                base += base_regs(c, 8, CG)
                for b in zs:
                    z_block(b, z_made, z_ok, zT_made)
                early(c + 1, 1)
                if c + 1 < NCH:
                    penalties(c + 1)
                if c == 0:
                    dve.wait_ge(acc_zeroed, 4)
                dve.wait_ge(open_all, c + 1)
                at = acc[0:F1, :, bass.ds(base[0], 1)]
                step(v.tensor_tensor(at, at, fb_ps.unsqueeze(2), ALU.mult))
                for g in range(sums_of(c)[-1][1]):
                    for i, (g0, _) in enumerate(sums_of(c)):
                        if g == g0:
                            dve.wait_ge(sums_made, 2 * c + i + 1)
                    at = acc[0:F1, :, bass.ds(base[g], WIN)]
                    w0 = (g % 8) * H * WIN
                    step(v.tensor_tensor(at, at, po[g // 8][0:F1, w0:w0 + H * WIN].rearrange("p (h w) -> p h w", h=H),
                                         ALU.add))
                    if g + 1 in [g1 for _, g1 in sums_of(c)]:
                        signal(sums_added)
                    if g == 7:
                        early(c + 1, 2)
            for b in range(ZIN, NZ):
                z_block(b, z_made, z_ok, zT_made)
            with if_flag(dve, ENG.DVE):
                def run(_):
                    dve.drain()

                run(v.memset(g_init[:, 0:H], -BIG))
                run(v.memset(g_init[:, H:SROW], 0.0))
                run(v.memset(g_e[:, F:F1], 1.0))
                signal(q_init)
                with dve.Fori(0, E // GT) as i:
                    dve.wait_ge(q_row, i * 16 + 16)
                    dve.wait_ge(q_old, i * 16 + 16)
                    run(v.tensor_copy(g_dstf, g_dst))
                    run(v.tensor_copy(g_row, g_row_i))
                    run(v.tensor_scalar(g_same, g_row, g_dstf, None, ALU.is_equal))
                    run(v.tensor_scalar(g_apart, g_row, g_dstf, -BIG, ALU.not_equal, ALU.mult))
                    dve.wait_ge(q_free, i + 1)
                    run(v.tensor_tensor(g_tmp, g_same, g_below, ALU.mult))
                    run(v.tensor_reduce(g_dup, g_tmp, AX.X, ALU.max))
                    run(v.scalar_tensor_tensor(g_to, g_dup, float(N), g_dstf, ALU.mult, ALU.add))
                    dve.wait_ge(q_h, i * 16 + 16)
                    dve.wait_ge(q_ea, i * 16 + 16)
                    run(v.tensor_tensor(g_e[:, 0:F], g_h, g_ea, ALU.add))
                    for hd in range(H):
                        run(v.tensor_tensor(g_prod, g_e[:, 0:F], wb[0:GT, hd, :], ALU.mult))
                        run(v.tensor_reduce(g_s[:, hd:hd + 1], g_prod, AX.X, ALU.add))
                    dve.wait_ge(q_er, i * 16 + 16)
                    run(v.tensor_tensor(g_s, g_s, g_er, ALU.add))
                    run(v.scalar_tensor_tensor(g_s, g_s, NEG_SLOPE, g_s, ALU.mult, ALU.max))
                    for hd in range(H):
                        run(v.tensor_scalar(g_diag[:, hd, :], ident[0:GT, 0:GT], g_s[:, hd:hd + 1], None, ALU.mult))
                    signal(q_diag)
                    dve.wait_ge(q_scores, i + 1)
                    run(v.tensor_tensor(g_sb, p_s[0:GT, 0:H * GT].rearrange("p (h e) -> p h e", h=H),
                                        view(g_apart, [[0, H], [1, GT]]), ALU.add))
                    run(v.tensor_reduce(g_mx, g_sb, AX.X, ALU.max))
                    dve.wait_ge(q_old, i * 16 + 16)
                    run(v.tensor_tensor(g_mx, g_mx, g_old[:, 0:H], ALU.max))
                    run(v.tensor_tensor(g_dif[:, 0:H], g_s, g_mx, ALU.subtract))
                    run(v.tensor_tensor(g_dif[:, H:2 * H], g_old[:, 0:H], g_mx, ALU.subtract))
                    signal(q_diff)
                    dve.wait_ge(q_exp, i + 1)
                    for hd in range(H):
                        run(v.tensor_scalar(g_u[:, hd, :], g_e, g_ex[:, hd:hd + 1], None, ALU.mult))
                    signal(q_terms)
                    run(v.tensor_copy(g_new[:, 0:H], g_mx))
                    dve.wait_ge(q_sum, i + 1)
                    for hd in range(H):
                        c0 = H + hd * F1
                        run(v.scalar_tensor_tensor(g_new[:, c0:c0 + F1], g_old[:, c0:c0 + F1], g_ex[:, H + hd:H + hd + 1],
                                                   p_m[0:GT, hd * F1:(hd + 1) * F1], ALU.mult, ALU.add))
                    signal(q_new)
                signal(q_state_ok)
                dve.wait_ge(zT_ok, NZ)
                with dve.Fori(0, N // GT) as b:
                    dve.wait_ge(q_state_turned, b + 2)
                    run(v.tensor_copy(acc[0:F1, :, bass.ds(b * GT, GT)],
                                      p_r[0:F1, 0:H * GT].rearrange("p (h n) -> p h n", h=H)))
                    signal(q_state_ok)
                signal(q_done)
                usual, done[:] = list(done), [r_steps, 0]
                step(v.memset(zmean[:, :, :], 0.0))
                step(v.memset(zdev[:, :, :], 0.0))
                for b in range(NZ):
                    z_block(b, r_made, r_ok, r_turned)
                done[:] = usual
            def over_r(t):
                step(v.tensor_tensor(zz[0:NP_], view(t[0:NP_, 0], [[0, NR], [1, F]]), view(t[0:NP_, 1], [[0, NR], [1, F]]),
                                     ALU.add))
                signal(bn_step)

            over_r(zmean)
            dm = zd[0:NP_]
            dve.wait_ge(bn_sum, 1)
            also(v.tensor_scalar(col[:, MU], p_s[:, F:F + 1], 1.0 / ZBL, None, ALU.mult))
            step(v.tensor_scalar(mu, p_s[:, 0:F], 1.0 / ZBL, None, ALU.mult))
            step(v.tensor_tensor(dm, zmean[0:NP_], view(mu[0:NP_], [[0, NR], [1, F]]), ALU.subtract))
            step(v.tensor_tensor(dm, dm, dm, ALU.mult))
            step(v.scalar_tensor_tensor(zdev[0:NP_], dm, float(NZ), zdev[0:NP_], ALU.mult, ALU.add))
            over_r(zdev)
            dve.wait_ge(bn_sum, 2)
            step(v.tensor_scalar(col[:, VAR], p_s[:, F + 1:F + 2], 1.0 / N, BN_EPS, ALU.mult, ALU.add))
            signal(bn_step)
            dve.wait_ge(bn_root, 1)
            step(v.reciprocal(col[:, REC], col[:, STD]))
            step(v.tensor_tensor(col[:, SCALE], col[:, REC], gb[:, 0:1], ALU.mult))
            step(v.tensor_tensor(col[:, REC], col[:, MU], col[:, SCALE], ALU.mult))
            step(v.tensor_tensor(col[:, SHIFT], gb[:, 1:2], col[:, REC], ALU.subtract))
            signal(bn_ok)
            dve.wait_ge(xres_in, 32)
            for n, (b0, b1) in enumerate(TURN):
                dve.wait_ge(z_back, n + 1)
                step(v.scalar_tensor_tensor(xres[0:NP_, b0:b1], view(out_banks[n % len(out_banks)][0:NP_, :],
                                                                     [[NR * F, b1 - b0], [1, NR * F]]), 0.0,
                                            xres[0:NP_, b0:b1], ALU.max, ALU.add))
                signal(y_ok)


_INS = ["x", "src", "dst", "edge_attr_64", "L0_gnn_W", "L0_gnn_attn_l", "L0_gnn_attn_r", "L0_gnn_bn_gamma",
        "L0_gnn_bn_beta"]


def kernel(**inputs):
    import numpy as _np
    import concourse.bacc as _bacc
    from concourse import mybir as _mybir
    from concourse.bass_utils import run_bass_kernel_spmd as _run

    nc = _bacc.Bacc("TRN2", target_bir_lowering=False, num_devices=1)
    arrays, args = {}, []
    for name in _INS:
        a = _np.ascontiguousarray(inputs[name])
        arrays[f"in_{name}"] = a
        args.append(nc.dram_tensor(f"in_{name}", a.shape, _mybir.dt.from_np(a.dtype), kind="ExternalInput").ap())
    args.append(nc.dram_tensor("out_0", (N, F), _mybir.dt.float32, kind="ExternalOutput").ap())
    gnn_kernel(nc, *args)
    r = _run(nc, [arrays], core_ids=[0])
    return r.results[0]["out_0"]
```
